# Optimizing a Trainium2 kernel written in Bass

```python
import numpy as np
import jax
import jax.numpy as jnp

def _softmax(x, axis=-1):
    return jax.nn.softmax(x, axis=axis)

def _gelu(x):
    return jax.nn.gelu(x, approximate=True)

def _silu(x):
    return jax.nn.silu(x)

def _sigmoid(x):
    return jax.nn.sigmoid(x)

def _layernorm(x, axis=-1, eps=1e-05):
    m = jnp.mean(x, axis=axis, keepdims=True)
    v = jnp.var(x, axis=axis, keepdims=True)
    return (x - m) / jnp.sqrt(v + eps)

def _scatter_add(tgt, idx, src, axis=0):
    return tgt.at[idx].add(src)

def _segment_sum(src, seg, n):
    return jax.ops.segment_sum(src, seg, n)
kernel_name = 'mk_recurrent_d1_jaxref_r8_34bced'

def setup_inputs(seed: int=0):
    np.random.seed(seed)
    _w = jnp.asarray

    def _L0_attn_setup():
        import jax, jax.numpy as jnp
        import numpy as np
        HIDDEN = 256
        KEY = 256
        EPS = 1e-05
        key = jax.random.key(seed)
        k1, k2, k3 = jax.random.split(key, 3)
        B, S = (4, 256)
        x = jax.random.normal(k1, (B, S, HIDDEN), dtype=jnp.float32)
        bq = 1.0 / np.sqrt(HIDDEN)
        qkv = jax.random.uniform(k2, (HIDDEN, KEY * 3), minval=-bq, maxval=bq, dtype=jnp.float32)
        bo = 1.0 / np.sqrt(KEY)
        o_proj = jax.random.uniform(k3, (KEY, HIDDEN), minval=-bo, maxval=bo, dtype=jnp.float32)
        gamma = jnp.ones((HIDDEN,), dtype=jnp.float32)
        beta = jnp.zeros((HIDDEN,), dtype=jnp.float32)
        return {'x': x, 'qkv': qkv, 'o_proj': o_proj, 'gamma': gamma, 'beta': beta}
    _L0_attn_in = _L0_attn_setup()

    def _L0_ffn_setup():
        import jax, jax.numpy as jnp
        import numpy as np
        B, S, H = (2, 64, 256)
        E, I, K = (64, 176, 6)
        NS = 2
        SH_I = I * NS
        key = jax.random.key(seed)
        ks = jax.random.split(key, 6)
        s = 0.02
        return {'hidden_states': jax.random.normal(ks[0], (B, S, H), jnp.float32), 'gate_w': jax.random.normal(ks[1], (E, H), jnp.float32) * s, 'experts_w1': jax.random.normal(ks[2], (E, I, H), jnp.float32) * s, 'experts_w2': jax.random.normal(ks[3], (E, H, I), jnp.float32) * s, 'shared_gate_up': jax.random.normal(ks[4], (2 * SH_I, H), jnp.float32) * s, 'shared_down': jax.random.normal(ks[5], (H, SH_I), jnp.float32) * s}
    _L0_ffn_in = _L0_ffn_setup()
    _d = {'L0_attn_x': _L0_attn_in['x'], 'L0_attn_qkv': _L0_attn_in['qkv'], 'L0_attn_o_proj': _L0_attn_in['o_proj'], 'L0_attn_gamma': _L0_attn_in['gamma'], 'L0_attn_beta': _L0_attn_in['beta'], 'L0_ffn_gate_w': _L0_ffn_in['gate_w'], 'L0_ffn_experts_w1': _L0_ffn_in['experts_w1'], 'L0_ffn_experts_w2': _L0_ffn_in['experts_w2'], 'L0_ffn_shared_gate_up': _L0_ffn_in['shared_gate_up'], 'L0_ffn_shared_down': _L0_ffn_in['shared_down']}
    _x0 = _d['L0_attn_x']
    _d['L0_attn_x'] = jax.random.normal(jax.random.fold_in(jax.random.key(seed), 1), (8, 256, 256), dtype=_x0.dtype)
    del _x0
    return _d

def reference(L0_attn_x, L0_attn_qkv, L0_attn_o_proj, L0_attn_gamma, L0_attn_beta, L0_ffn_gate_w, L0_ffn_experts_w1, L0_ffn_experts_w2, L0_ffn_shared_gate_up, L0_ffn_shared_down):

    def _L0_attn_ref(x, qkv, o_proj, gamma, beta):
        import jax, jax.numpy as jnp
        import numpy as np
        HIDDEN = 256
        KEY = 256
        EPS = 1e-05
        residual = x
        mu = jnp.mean(x, axis=-1, keepdims=True)
        var = jnp.mean((x - mu) ** 2, axis=-1, keepdims=True)
        x_norm = (x - mu) / jnp.sqrt(var + EPS) * gamma + beta
        q = x_norm @ qkv[:, :KEY]
        k = x_norm @ qkv[:, KEY:2 * KEY]
        v = x_norm @ qkv[:, 2 * KEY:]
        scale = 1.0 / jnp.sqrt(jnp.float32(KEY))
        scores = jnp.einsum('bsk,btk->bst', q, k) * scale
        S_len = x.shape[1]
        causal = jnp.tril(jnp.ones((S_len, S_len), dtype=bool))
        scores = jnp.where(causal[None], scores, -jnp.inf)
        attn = jax.nn.softmax(scores, axis=-1)
        out = attn @ v
        out = out @ o_proj
        return out + residual

    def _L0_ffn_ref(hidden_states, gate_w, experts_w1, experts_w2, shared_gate_up, shared_down):
        import jax, jax.numpy as jnp
        import numpy as np
        B, S, H = (2, 64, 256)
        E, I, K = (64, 176, 6)
        NS = 2
        SH_I = I * NS
        orig_shape = hidden_states.shape
        x = hidden_states.reshape(-1, orig_shape[-1])
        router_logits = x @ gate_w.T
        probs = jax.nn.softmax(router_logits, axis=-1)
        topk_w, topk_idx = jax.lax.top_k(probs, K)
        topk_w = topk_w / jnp.sum(topk_w, axis=-1, keepdims=True)
        combine = jnp.sum(jax.nn.one_hot(topk_idx, E, dtype=x.dtype) * topk_w[..., None], axis=1)
        h = jax.nn.silu(jnp.einsum('th,eih->tei', x, experts_w1))
        y = jnp.einsum('tei,ehi->teh', h, experts_w2)
        routed_out = jnp.einsum('teh,te->th', y, combine)
        gu = x @ shared_gate_up.T
        g, u = jnp.split(gu, 2, axis=-1)
        shared_out = jax.nn.silu(g) * u @ shared_down.T
        return (routed_out + shared_out).reshape(orig_shape)
    x = L0_attn_x
    xn = _layernorm(x, axis=-1)
    s = _L0_attn_ref(xn, L0_attn_qkv, L0_attn_o_proj, L0_attn_gamma, L0_attn_beta)
    g = _silu(_L0_ffn_ref(xn, L0_ffn_gate_w, L0_ffn_experts_w1, L0_ffn_experts_w2, L0_ffn_shared_gate_up, L0_ffn_shared_down))
    x = x + s * g
    return x

_drawn_inputs = setup_inputs


def setup_inputs(seed=0):
    import zlib

    import numpy as np

    out = dict(_drawn_inputs(seed))
    spreads = {'L0_attn_gamma': (1.0, 0.6), 'L0_attn_beta': (0.0, 0.8)}
    factors = {'L0_attn_qkv': 8.0,
     'L0_attn_o_proj': 8.0,
     'L0_ffn_gate_w': 6.305,
     'L0_ffn_experts_w1': 5.911,
     'L0_ffn_experts_w2': 5.885,
     'L0_ffn_shared_gate_up': 5.643,
     'L0_ffn_shared_down': 5.642}
    for name, (base, spread) in spreads.items():
        noise = np.random.default_rng([zlib.crc32(name.encode()), seed]).standard_normal(out[name].shape)
        drawn = base * np.exp(spread * noise) if base else spread * noise
        out[name] = jnp.asarray(drawn.astype(out[name].dtype))
    for name, factor in factors.items():
        out[name] = (out[name] * factor).astype(out[name].dtype)
    return out
```

```python
from contextlib import ExitStack

import concourse.bass as bass
from concourse import mybir

F32 = mybir.dt.float32
F16 = mybir.dt.float16
BF16 = mybir.dt.bfloat16
I32 = mybir.dt.int32
U32 = mybir.dt.uint32
ALU = mybir.AluOpType
ACT = mybir.ActivationFunctionType
AX_X = mybir.AxisListType.X

P = 128


def gated_moe_attention(nc, x, qkv_t, o_proj, gamma_beta, gate_t, w1_t, w2_main, w2_rest,
                        shared_up_t, shared_down_t, out):
    T, H = x.shape
    E, _, HC, I = w1_t.shape
    NT = T // P
    NB = 8
    S = T // NB
    K = 6
    SLOTS = 256
    ROUNDS = T // SLOTS
    IR = I - P
    SI = shared_down_t.shape[0]
    SC = (SI + P - 1) // P
    SW = [min(P, SI - m * P) for m in range(SC)]
    GROUPS, GT = 4, NT // 4
    RA = 16
    EG = 8
    BIG = 16384
    EPS = 1e-5
    SCALE = float(H) ** -0.5
    PAD, GONE = -1.0e38, -3.0e38
    ROUND_ROWS = E * SLOTS
    ABOVE = 4.0 * ROUND_ROWS

    xn_rows = nc.dram_tensor("xn_rows", [T, H], F32, kind="Internal").ap()
    token_lists = nc.dram_tensor("token_lists", [P, P], F32, kind="Internal").ap()
    y_rows = nc.dram_tensor("y_rows", [ROUND_ROWS, H], F32, kind="Internal").ap()

    with ExitStack() as ctx:
        def sb(name, shape, dt=F32):
            return ctx.enter_context(nc.sbuf_tensor(name, [P] + shape, dt))

        def sem(name):
            return ctx.enter_context(nc.semaphore(name))

        def sems(name):
            return [sem(f"{name}{i}") for i in range(2)]

        bank = [ctx.enter_context(nc.psum_tensor(f"bank{i}", [P, 512], F32)) for i in range(8)]

        ident = sb("ident", [P])
        before = sb("before", [P], BF16)
        ones = sb("ones", [P], BF16)
        iota_a = sb("iota_a", [RA, EG], F16)
        iota_b = sb("iota_b", [RA, EG], F16)
        token_no = sb("token_no", [NT])
        expert_row = sb("expert_row", [E], I32)
        same_expert = sb("same_expert", [EG])
        causal = sb("causal", [3 * P])
        minus_half = sb("minus_half", [NT])
        round_a = sb("round_a", [ROUNDS])
        round_q = sb("round_q", [ROUNDS])

        gb = sb("gb", [2, HC])
        gate_sb = sb("gate_sb", [HC, E])
        wqk = sb("wqk", [HC, H])
        wvo = sb("wvo", [HC, H])
        up_sb = sb("up_sb", [HC, 2 * SI])
        down_sb = sb("down_sb", [SC, H])

        x_all = sb("x_all", [NT, H])
        xn_all = sb("xn_all", [NT, H])
        xn_t = sb("xn_t", [HC, T])
        stats = sb("stats", [GT, 6])
        mean_var = sb("mean_var", [NT, 2])
        rstd = sb("rstd", [NT])
        var_eps = sb("var_eps", [NT])

        logits = sb("logits", [NT, E + 2])
        left = sb("left", [GT, E + 2])
        top8 = sb("top8", [NT, 8])
        taken = sb("taken", [NT, 8])
        neg_max = sb("neg_max", [NT])
        exp_all = sb("exp_all", [NT, E])
        chosen = sb("chosen", [NT, E], BF16)
        chosen_before = sb("chosen_before", [NT + 1, E], BF16)
        most = sb("most", [1])
        most_int = sb("most_int", [1], I32)
        rank_int = sb("rank_int", [NT * E], I32)
        rank_a = sb("rank_a", [NT, E], F16)
        rank_b = sb("rank_b", [NT, E], F16)
        round_rank_a = sb("round_rank_a", [NT, E], F16)
        space_a = sb("space_a", [NT * RA * E // 2])
        space_b = sb("space_b", [NT * RA * E // 2])
        hot_a = space_a[:].bitcast(F16).rearrange("p (t g a e) -> p t g a e", t=NT, a=RA, e=EG)
        hot_b = space_b[:].bitcast(F16).rearrange("p (t g b e) -> p t g b e", t=NT, b=RA, e=EG)
        qkv_sb = space_a[:, 0:3 * HC * H].rearrange("p (w c d) -> p w c d", w=3, c=HC)
        o_sb = space_a[:, 3 * HC * H:4 * HC * H].rearrange("p (c d) -> p c d", c=HC)
        own = sb("own", [8 * P])
        int_a = own[:].bitcast(I32)
        lists = sb("lists", [P])
        lists_by_expert = sb("lists_by_expert", [SLOTS])
        slot_token = sb("slot_token", [2, E], U32)
        f_q = sb("f_q", [E], I32)
        f_slot = sb("f_slot", [E], I32)
        f_round_w = sb("f_round_w", [E])
        f_w = sb("f_w", [E])
        f_sum = sb("f_sum", [1])
        f_inv = sb("f_inv", [1])
        f_k1 = sb("f_k1", [E])
        f_key = sb("f_key", [E])
        f_top = sb("f_top", [8])
        f_hit = sb("f_hit", [K, E])
        f_wk = sb("f_wk", [8])
        f_stats = sb("f_stats", [6])
        f_mean_var = sb("f_mean_var", [2])
        weight = sb("weight", [NT, 8])
        y_row = sb("y_row", [NT, 8], U32)
        mean_var2 = sb("mean_var2", [NT, 2])
        rstd2 = sb("rstd2", [NT])

        extra = sb("extra", [NT, H])

        w1_sb = [sb(f"w1_sb{i}", [HC, I]) for i in range(2)]
        w2_sb = [sb(f"w2_sb{i}", [H]) for i in range(2)]
        w2r_sb = [sb(f"w2r_sb{i}", [2, H]) for i in range(2)]
        idx_sb = [sb(f"idx_sb{i}", [2], U32) for i in range(2)]
        xg = [sb(f"xg{i}", [2, H]) for i in range(2)]
        xg_t = [sb(f"xg_t{i}", [HC, SLOTS]) for i in range(2)]
        th = [sb(f"th{i}", [3 * P]) for i in range(2)]
        hid = [sb(f"hid{i}", [3 * P]) for i in range(2)]
        y_sb = [sb(f"y_sb{i}", [2, H]) for i in range(2)]

        used = {0: 0, 1: 0}

        def room(which, n):
            space = (space_a, space_b)[which]
            start = used[which]
            used[which] = start + n
            assert used[which] <= NT * RA * E // 2
            return space[:, start:start + n]

        yg = [room(0, 2 * K * H).rearrange("p (s k d) -> p s k d", s=2, k=K) for _ in range(2)]
        z_sb = room(0, 2 * H).rearrange("p (s d) -> p s d", s=2)
        z_t = room(0, HC * S).rearrange("p (c s) -> p c s", c=HC)
        g_t = room(0, HC * S).rearrange("p (c s) -> p c s", c=HC)
        vo = room(1, 2 * H).rearrange("p (s d) -> p s d", s=2)
        scores = room(1, 3 * P)
        probs = room(1, 3 * P)
        probs_t = room(1, 3 * P)
        tg = [room(1, S) for _ in range(2)]
        hg = [room(1, S) for _ in range(2)]
        hs = room(1, SC * S).rearrange("p (m s) -> p m s", m=SC)
        routed = room(1, 2 * H).rearrange("p (s d) -> p s d", s=2)
        ffn = room(1, 2 * H)
        ffn_th = room(1, 2 * H)
        att = room(1, 2 * H)
        gated = room(1, 2 * H)
        out_sb = [room(1, 2 * H) for _ in range(2)]
        row_max = sb("row_max", [2])
        row_bias = sb("row_bias", [2])
        row_sum = sb("row_sum", [2])
        row_inv = sb("row_inv", [2])
        yi_sb = [sb(f"yi_sb{i}", [2, 8], U32) for i in range(2)]
        wk_sb = sb("wk_sb", [2, 8])

        x_in = [sem(f"x_in{g}") for g in range(GROUPS)]
        qkv_in, o_in, gb_in, gate_in, up_in = sem("qkv_in"), sem("o_in"), sem("gb_in"), sem("gate_in"), sem("up_in")
        pool_const, dve_const = sem("pool_const"), sem("dve_const")
        const_ready = sem("const_ready")
        wqk_done, wqk_ready = sem("wqk_done"), sem("wqk_ready")
        ln_step, var_ready, rstd_step, rstd_ready = sem("ln_step"), sem("var_ready"), sem("rstd_step"), sem("rstd_ready")
        xn_ready, xn_stored = sem("xn_ready"), sem("xn_stored")
        xnt_done, xnt_ready = sem("xnt_done"), sem("xnt_ready")
        logits_done, logits_ready, top_ready = sem("logits_done"), sem("logits_ready"), sem("top_ready")
        route_step, chosen_ready, exp_ready = sem("route_step"), sem("chosen_ready"), sem("exp_ready")
        before_step, rank_done = sem("before_step"), sem("rank_done")
        count_read, most_ready, rank_step, rank_ready = sem("count_read"), sem("most_ready"), sem("rank_step"), sem("rank_ready")
        hot_b_ready, hot_b_scaled, hot_a_ready, hot_a_read = sem("hot_b_ready"), sem("hot_b_scaled"), sem("hot_a_ready"), sem("hot_a_read")
        own_step, lists_ready, lists_stored, lists_in = sem("own_step"), sem("lists_ready"), sem("lists_stored"), sem("lists_in")
        lists_t_done, slots_ready = sem("lists_t_done"), sem("slots_ready")
        idx_ready, xg_in, xg_t_done, xg_t_ready = sems("idx_ready"), sems("xg_in"), sems("xg_t_done"), sems("xg_t_ready")
        w1_in, w2_in = sems("w1_in"), sems("w2_in")
        up_done, th_ready, hid_ready, y_done, y_ready, y_stored = (sems(n) for n in ("up_done", "th_ready", "hid_ready", "y_done", "y_ready", "y_stored"))
        fin_step, fin_done = sem("fin_step"), sem("fin_done")
        rounds_done, extra_idx_ready, extra_in, extra_step, extra_done = (
            sem(n) for n in ("rounds_done", "extra_idx_ready", "extra_in", "extra_step", "extra_done"))
        round_stored = sem("round_stored")
        gathers_begun, stores_begun, hot_a_begun = sem("gathers_begun"), sem("stores_begun"), sem("hot_a_begun")
        rstd2_ready, rstd2_step = sem("rstd2_ready"), sem("rstd2_step")
        yi_ready, yg_in, yg_used = sems("yi_ready"), sems("yg_in"), sems("yg_used")
        z_ready, zt_done, zt_ready = sem("z_ready"), sem("zt_done"), sem("zt_ready")
        gt_done, gt_ready, vo_done, vo_ready = sem("gt_done"), sem("gt_ready"), sem("vo_done"), sem("vo_ready")
        scores_done, scores_step, bias_ready, probs_ready = sem("scores_done"), sem("scores_step"), sem("bias_ready"), sem("probs_ready")
        inv_ready, pt_done, pt_ready, pv_done, pv_read = sem("inv_ready"), sem("pt_done"), sem("pt_ready"), sem("pv_done"), sem("pv_read")
        gu_done, tg_ready, hg_step, hs_ready = sem("gu_done"), sem("tg_ready"), sem("hg_step"), sem("hs_ready")
        down_done, routed_step, ffn_ready, ffn_th_ready = sem("down_done"), sem("routed_step"), sem("ffn_ready"), sem("ffn_th_ready")
        final_step, out_ready, out_stored = sem("final_step"), sems("out_ready"), sems("out_stored")

        x_tiles = x.rearrange("(t p) d -> p t d", p=P)
        xn_tiles = xn_rows.rearrange("(t p) d -> p t d", p=P)
        out_tiles = out.rearrange("(t p) d -> p t d", p=P)

        block = ctx.enter_context(nc.Block())

        def rounds(eng, body, between=None):
            eng.wait_ge(most_ready, 1)
            n = eng.value_load(most_int[0:1, 0:1], min_val=1, max_val=T)
            with eng.Fori(0, ROUNDS) as r:
                with eng.If(r * SLOTS < n):
                    q = nc.s_assert_within((n - 1) // SLOTS - r, 0, ROUNDS - 1,
                                           skip_runtime_bounds_check_because="r * SLOTS < n <= T in this branch")
                    body(r, q)
                if between:
                    with eng.If((r + 1) * SLOTS < n):
                        between(r)

        def batches(eng, body):
            body(0, 0)
            with eng.Fori(0, NB // 2 - 1) as j:
                body(2 * j + 1, 1)
                body(2 * j + 2, 0)
            body(NB - 1, 1)

        @block.sync
        def _(sp):
            for g in range(GROUPS):
                sp.dma_start(x_all[:, g * GT:(g + 1) * GT, :], x_tiles[:, g * GT:(g + 1) * GT, :]).then_inc(x_in[g], 16)
            sp.dma_start(up_sb[:], shared_up_t).then_inc(up_in, 16)
            for m in range(SC):
                sp.dma_start(down_sb[0:SW[m], m, :], shared_down_t[m * P:m * P + SW[m], :]).then_inc(up_in, 16)
            for g in range(GROUPS):
                sp.wait_ge(xn_ready, g + 1)
                sp.dma_start(xn_tiles[:, g * GT:(g + 1) * GT, :], xn_all[:, g * GT:(g + 1) * GT, :]).then_inc(xn_stored, 16)

            def load_w1(e, i, n):
                sp.wait_ge(up_done[i], n)
                sp.dma_start(w1_sb[i][:], w1_t[bass.ds(e, 1), :, :, :].rearrange("o p c i -> (o p) c i")).then_inc(w1_in[i], 16)

            def load_w2(e, i, n):
                sp.wait_ge(y_done[i], n)
                sp.dma_start(w2_sb[i][:], w2_main[bass.ds(e, 1), :, :].rearrange("o p d -> (o p) d")).then_inc(w2_in[i], 16)
                rest = w2_rest[bass.ds(e, 1), :, :].rearrange("o p d -> (o p) d")
                sp.dma_start(w2r_sb[i][0:IR, 0, :], rest).then_inc(w2_in[i], 16)
                sp.dma_start(w2r_sb[i][64:64 + IR, 1, :], rest).then_inc(w2_in[i], 16)

            def store_y(e, i, n):
                sp.wait_ge(y_ready[i], n + 1)
                rows = y_rows[bass.ds(e * SLOTS, SLOTS), :].rearrange("(t p) d -> p t d", p=P)
                sp.dma_start(rows, y_sb[i][:]).then_inc(y_stored[i], 16)

            def one_round(r, q):
                n0 = r * (E // 2)
                load_w1(0, 0, n0)
                load_w2(0, 0, n0)
                load_w1(1, 1, n0)
                load_w2(1, 1, n0)
                sp.wait_ge(lists_ready, r + 1)
                sp.dma_start(token_lists, lists[:]).then_inc(lists_stored, 16)
                sp.wait_ge(lists_stored, 16 * r + 16)
                for g in range(E // EG):
                    sp.dma_start(lists_by_expert[g * EG:(g + 1) * EG, :].rearrange("e (a b) -> e a b", a=RA),
                                 token_lists[:, g * RA:(g + 1) * RA].rearrange("(a e) b -> e a b", e=EG)).then_inc(lists_in, 16)
                sp.wait_ge(extra_done, NT * r)
                sp.sem_inc(stores_begun, 1)
                with sp.Fori(0, E // 2 - 1) as j:
                    for i in range(2):
                        load_w1(2 * j + 2 + i, i, n0 + j + 1)
                        store_y(2 * j + i, i, n0 + j)
                        load_w2(2 * j + 2 + i, i, n0 + j + 1)
                for i in range(2):
                    store_y(E - 2 + i, i, n0 + E // 2 - 1)
                sp.wait_ge(xn_stored, 16 * GROUPS)
                for i in range(2):
                    sp.wait_ge(y_stored[i], 16 * (n0 + E // 2))
                sp.sem_inc(round_stored, 1)

            rounds(sp, one_round)
            sp.sem_inc(rounds_done, 1)

            with sp.Fori(0, NB // 2) as j:
                for i in range(2):
                    sp.wait_ge(out_ready[i], j + 1)
                    sp.dma_start(out_tiles[:, bass.ds(2 * (2 * j + i), 2), :],
                                 out_sb[i].rearrange("p (s d) -> p s d", s=2)).then_inc(out_stored[i], 16)
            for i in range(2):
                sp.wait_ge(out_stored[i], 16 * (NB // 2))
            sp.wait_ge(xn_stored, 16 * GROUPS)

        @block.gpsimd
        def _(pool):
            pool.memset(ident[:], 0.0).then_inc(pool_const, 1)
            pool.memset(ones[:], 1.0).then_inc(pool_const, 1)
            pool.memset(before[:], 1.0).then_inc(pool_const, 1)
            pool.memset(causal[:], 0.0).then_inc(pool_const, 1)
            pool.memset(minus_half[:], -0.5).then_inc(pool_const, 1)
            pool.memset(chosen_before[:, 0, :], 0.0).then_inc(pool_const, 1)
            pool.wait_ge(pool_const, 6)
            pool.affine_select(out=ident[:], in_=ident[:], compare_op=ALU.not_equal, fill=1.0, base=0,
                               pattern=[[-1, P]], channel_multiplier=1).then_inc(const_ready, 1)
            pool.affine_select(out=before[:], in_=before[:], compare_op=ALU.is_gt, fill=0.0, base=0,
                               pattern=[[1, P]], channel_multiplier=-1).then_inc(const_ready, 1)
            for m in (0, 2):
                pool.affine_select(out=causal[:, m * P:(m + 1) * P], in_=causal[:, m * P:(m + 1) * P],
                                   compare_op=ALU.is_ge, fill=-1.0e30, base=0,
                                   pattern=[[-1, P]], channel_multiplier=1).then_inc(const_ready, 1)

            def rstd_of(g):
                ts = slice(g * GT, (g + 1) * GT)
                pool.wait_ge(var_ready, g + 1)
                pool.tensor_scalar(var_eps[:, ts], mean_var[:, ts, 1], EPS, None, ALU.add).then_inc(rstd_step, 1)
                pool.wait_ge(rstd_step, g + 1)
                pool.tensor_tensor(rstd[:, ts], var_eps[:, ts], minus_half[:, ts], ALU.pow).then_inc(rstd_ready, 1)

            for g in range(GROUPS):
                rstd_of(g)
            pool.iota(int_a[:, 0:P], [[1, RA], [0, EG]], base=-(BIG // RA), channel_multiplier=0).then_inc(const_ready, 1)
            pool.iota(rank_int[:, 0:P], [[1, RA], [0, EG]], base=0, channel_multiplier=0).then_inc(const_ready, 1)
            pool.iota(expert_row[:], [[SLOTS, E]], base=0, channel_multiplier=0).then_inc(const_ready, 1)
            pool.iota(int_a[:, P:P + NT], [[P, NT]], base=0, channel_multiplier=1).then_inc(const_ready, 1)

            pool.iota(int_a[:, 2 * P:2 * P + ROUNDS], [[SLOTS // RA, ROUNDS]], base=0, channel_multiplier=0).then_inc(const_ready, 1)
            pool.iota(int_a[:, 3 * P:3 * P + ROUNDS], [[1, ROUNDS]], base=-(BIG // SLOTS),
                      channel_multiplier=0).then_inc(const_ready, 1)

            for t in range(NT):
                if t % GT == 0:
                    pool.wait_ge(chosen_ready, t // GT + 1)
                if t:
                    pool.wait_ge(before_step, t)
                pool.tensor_tensor(chosen_before[:, t + 1, :], chosen_before[:, t, :], chosen[:, t, :],
                                   ALU.add).then_inc(before_step, 1)

            def gather_x(e, i, n):
                pool.wait_ge(xg_in[i], 32 * n)
                pool.tensor_copy(idx_sb[i][:], slot_token[:, :, bass.ds(e, 1)].rearrange("p h o -> p (h o)")).then_inc(idx_ready[i], 1)
                pool.wait_ge(idx_ready[i], n + 1)
                pool.wait_ge(xg_t_done[i], n)
                pool.sem_inc(gathers_begun, 1)
                for h in range(2):
                    pool.indirect_dma_start(xg[i][:, h, :], None, xn_rows,
                                            bass.IndirectOffsetOnAxis(ap=idx_sb[i][:, h:h + 1], axis=0)).then_inc(xg_in[i], 16)

            def one_round(r, q):
                pool.wait_ge(xn_stored, 16 * GROUPS)
                pool.wait_ge(slots_ready, r + 1)
                pool.sem_inc(gathers_begun, 1)
                with pool.Fori(0, E // 2) as j:
                    for i in range(2):
                        gather_x(2 * j + i, i, r * (E // 2) + j)

            def gather_extra(r):
                with pool.Fori(0, NT) as t:
                    n = r * NT + t
                    pool.wait_ge(extra_in, K * 16 * n)
                    pool.tensor_copy(yi_sb[0][:, 0:1, :], y_row[:, bass.ds(t, 1), :]).then_inc(extra_idx_ready, 1)
                    pool.wait_ge(extra_idx_ready, n + 1)
                    pool.wait_ge(round_stored, r + 1)
                    pool.wait_ge(extra_done, n)
                    pool.sem_inc(gathers_begun, 1)
                    for k in range(K):
                        pool.indirect_dma_start(yg[0][:, 0, k, :], None, y_rows,
                                                bass.IndirectOffsetOnAxis(ap=yi_sb[0][:, 0, k:k + 1], axis=0)).then_inc(extra_in, 16)

            rounds(pool, one_round, gather_extra)

            pool.wait_ge(fin_done, 1)
            pool.tensor_scalar(var_eps[:], mean_var2[:, :, 1], EPS, None, ALU.add).then_inc(rstd2_step, 1)
            pool.wait_ge(rstd2_step, 1)
            pool.tensor_tensor(rstd2[:], var_eps[:], minus_half[:], ALU.pow).then_inc(rstd2_ready, 1)
            pool.wait_ge(rounds_done, 1)
            with pool.Fori(0, NB // 2) as j:
                for i in range(2):
                    pool.wait_ge(yg_in[i], 2 * K * 16 * j)
                    pool.tensor_copy(yi_sb[i][:], y_row[:, bass.ds(2 * (2 * j + i), 2), :]).then_inc(yi_ready[i], 1)
                    pool.wait_ge(yi_ready[i], j + 1)
                    pool.wait_ge(yg_used[i], j)
                    pool.sem_inc(gathers_begun, 1)
                    for s in range(2):
                        for k in range(K):
                            pool.indirect_dma_start(yg[i][:, s, k, :], None, y_rows,
                                                    bass.IndirectOffsetOnAxis(ap=yi_sb[i][:, s, k:k + 1], axis=0)).then_inc(yg_in[i], 16)

        def exps(act, g):
            act.wait_ge(top_ready, g + 1)
            for t in range(g * GT, (g + 1) * GT):
                ins = act.activation(exp_all[:, t, :], logits[:, t, 0:E], ACT.Exp, bias=neg_max[:, t:t + 1])
            ins.then_inc(exp_ready, 1)

        @block.scalar
        def _(act):
            act.dma_start(gate_sb[:], gate_t).then_inc(gate_in, 16)
            act.dma_start(qkv_sb, qkv_t).then_inc(qkv_in, 16)
            act.dma_start(o_sb, o_proj.rearrange("(c p) n -> p c n", p=P)).then_inc(o_in, 16)
            act.dma_start(gb[:], gamma_beta).then_inc(gb_in, 16)

            for w, dst in enumerate((wqk, wvo)):
                act.wait_ge(wqk_done, w + 1)
                act.copy(dst[:].rearrange("p c n -> p (c n)"), bank[6 + w][:]).then_inc(wqk_ready, 1)

            for g in range(GROUPS):
                for u in range(2):
                    act.wait_ge(xnt_done, 2 * g + u + 1)
                    t = g * GT + 2 * u
                    act.copy(xn_t[:, :, t * P:(t + 2) * P], bank[u][:].rearrange("p (c s) -> p c s", c=HC)).then_inc(xnt_ready, 1)
                if g:
                    exps(act, g - 1)
            exps(act, GROUPS - 1)

            with act.Fori(0, NT) as t:
                act.wait_ge(hot_b_ready, t + 1)
                act.activation(hot_b[:, bass.ds(t, 1), :, :, :].rearrange("p o g b e -> p (o g b e)"),
                               hot_b[:, bass.ds(t, 1), :, :, :].rearrange("p o g b e -> p (o g b e)"), ACT.Copy,
                               scale=token_no[:, bass.ds(t, 1)]).then_inc(hot_b_scaled, 1)

            def expert(i, n):
                act.wait_ge(xg_t_done[i], n + 1)
                act.wait_ge(up_done[i], n)
                act.copy(xg_t[i][:].rearrange("p c s -> p (c s)"), bank[i][:]).then_inc(xg_t_ready[i], 1)
                act.wait_ge(up_done[i], n + 1)
                act.wait_ge(hid_ready[i], n)
                act.activation(th[i][:], bank[2 + i][:, 0:3 * P], ACT.Tanh, scale=0.5).then_inc(th_ready[i], 1)

            def one_round(r, q):
                with act.Fori(0, E // 2) as j:
                    for i in range(2):
                        expert(i, r * (E // 2) + j)

            rounds(act, one_round)

            def z_evac(b):
                act.wait_ge(zt_done, b + 1)
                act.wait_ge(scores_done, b)
                for c in range(HC):
                    ins = act.activation(z_t[:, c, :], bank[0][:, c * S:(c + 1) * S], ACT.Identity,
                                         bias=gb[:, 1, c:c + 1], scale=gb[:, 0, c:c + 1])
                ins.then_inc(zt_ready, 1)

            def batch(b, i):
                act.wait_ge(gt_done, b + 1)
                act.copy(g_t.rearrange("p c s -> p (c s)"), bank[1][:]).then_inc(gt_ready, 1)
                act.wait_ge(vo_done, b + 1)
                act.wait_ge(pv_done, b)
                act.copy(vo.rearrange("p s d -> p (s d)"), bank[2][:]).then_inc(vo_ready, 1)
                act.wait_ge(bias_ready, b + 1)
                act.wait_ge(pt_done, b)
                act.wait_ge(inv_ready, b)
                act.activation(probs[:, 0:P], scores[:, 0:P], ACT.Exp, bias=row_bias[:, 0:1], scale=SCALE,
                               accum_out=row_sum[:, 0:1])
                act.activation(probs[:, P:3 * P], scores[:, P:3 * P], ACT.Exp, bias=row_bias[:, 1:2], scale=SCALE,
                               accum_out=row_sum[:, 1:2]).then_inc(probs_ready, 1)
                for m in range(SC):
                    if m == 2 and not (isinstance(b, int) and b == 0):
                        ffn_tanh(b - 1)
                    c = (SC * i + m) % 2
                    act.wait_ge(gu_done, SC * b + m + 1)
                    if not (isinstance(b, int) and b == 0 and m < 2):
                        act.wait_ge(hs_ready, SC * b + m - 1)
                    act.activation(tg[c][0:SW[m], :], bank[4 + c][0:SW[m], 0:S], ACT.Tanh, scale=0.5).then_inc(tg_ready, 1)
                act.wait_ge(pt_done, b + 1)
                act.copy(probs_t, bank[0][:, 0:3 * P]).then_inc(pt_ready, 1)
                if not (isinstance(b, int) and b == NB - 1):
                    z_evac(b + 1)

            def ffn_tanh(b):
                act.wait_ge(ffn_ready, b + 1)
                act.activation(ffn_th, ffn, ACT.Tanh, scale=0.5).then_inc(ffn_th_ready, 1)

            act.wait_ge(gb_in, 16)
            z_evac(0)
            batches(act, batch)
            ffn_tanh(NB - 1)

        @block.vector
        def _(dve):
            dve.memset(logits[:, :, E:E + 2], PAD).then_inc(dve_const, 1)
            dve.memset(taken[:, :, K:8], PAD).then_inc(dve_const, 1)
            for i in range(2):
                dve.memset(w2r_sb[i][:], 0.0).then_inc(dve_const, 1)
                dve.memset(bank[2 + i][:], 0.0).then_inc(dve_const, 1)
            dve.memset(lists_by_expert[:], 0.0).then_inc(dve_const, 1)
            N_CONST = 7
            ln = [0]

            def statistics(g):
                dve.wait_ge(x_in[g], 16)
                for i in range(GT):
                    ins = dve.bn_stats(stats[:, i, :], x_all[:, g * GT + i, :])
                ins.then_inc(ln_step, 1)
                ln[0] += 1
                dve.wait_ge(ln_step, ln[0])
                for i in range(GT):
                    ins = dve.bn_aggr(mean_var[:, g * GT + i, :], stats[:, i, :])
                ins.then_inc(var_ready, 1)
                dve.wait_ge(var_ready, g + 1)

            def normalise(g):
                dve.wait_ge(rstd_ready, g + 1)
                for t in range(g * GT, (g + 1) * GT):
                    ins = dve.tensor_scalar(xn_all[:, t, :], x_all[:, t, :], mean_var[:, t, 0:1], rstd[:, t:t + 1],
                                            ALU.subtract, ALU.mult)
                ins.then_inc(xn_ready, 1)

            def by_group(ranks, t):
                return (ranks[:, bass.ds(t, 1), :].rearrange("p o (g e) -> p (o g) e", e=EG).unsqueeze(2)
                        .broadcast_to([P, E // EG, RA, EG]))

            rs = [0]

            def step(ins):
                rs[0] += 1
                ins.then_inc(route_step, 1)
                dve.wait_ge(route_step, rs[0])

            def route(g):
                ts = slice(g * GT, (g + 1) * GT)
                dve.wait_ge(logits_done, g + 1)
                dve.tensor_copy(logits[:, ts, 0:E], bank[2 + g % 2][:, 0:GT * E].rearrange("p (t e) -> p t e", e=E)).then_inc(logits_ready, 1)
                dve.wait_ge(logits_ready, g + 1)
                for t in range(g * GT, (g + 1) * GT):
                    ins = dve.max(top8[:, t, :], logits[:, t, 0:E])
                step(ins)
                dve.tensor_scalar(neg_max[:, ts], top8[:, ts, 0], -1.0, None, ALU.mult).then_inc(top_ready, 1)
                step(dve.tensor_copy(taken[:, ts, 0:K], top8[:, ts, 0:K]))
                for i in range(GT):
                    ins = dve.match_replace(left[:, i, :], taken[:, g * GT + i, :], logits[:, g * GT + i, :], GONE)
                step(ins)
                dve.tensor_tensor(chosen[:, ts, :], left[:, :, 0:E], logits[:, ts, 0:E], ALU.not_equal).then_inc(chosen_ready, 1)

            dve.wait_ge(dve_const, N_CONST)
            statistics(0)
            statistics(1)
            normalise(0)
            statistics(2)
            normalise(1)
            route(0)
            statistics(3)
            normalise(2)
            route(1)
            normalise(3)
            dve.wait_ge(const_ready, 10)
            dve.tensor_copy(iota_a[:].rearrange("p a e -> p (a e)"), int_a[:, 0:P]).then_inc(dve_const, 1)
            dve.tensor_copy(iota_b[:].rearrange("p a e -> p (a e)"), rank_int[:, 0:P]).then_inc(dve_const, 1)
            dve.tensor_copy(token_no[:], int_a[:, P:P + NT]).then_inc(dve_const, 1)
            dve.tensor_copy(round_a[:], int_a[:, 2 * P:2 * P + ROUNDS]).then_inc(dve_const, 1)
            dve.tensor_copy(round_q[:], int_a[:, 3 * P:3 * P + ROUNDS]).then_inc(dve_const, 1)
            dve.memset(extra[:], 0.0).then_inc(dve_const, 1)
            dve.tensor_reduce(same_expert[:], ident[:].rearrange("p (a e) -> p e a", a=RA), AX_X, ALU.add).then_inc(dve_const, 1)
            route(2)
            route(3)

            dve.wait_ge(dve_const, N_CONST + 7)
            for h in range(2):
                dve.wait_ge(rank_done, h + 1)
                half = slice(h * 512, (h + 1) * 512)
                dve.scalar_tensor_tensor(out=rank_int[:, half],
                                         in0=chosen[:, h * 8:(h + 1) * 8, :].rearrange("p t e -> p (t e)"),
                                         scalar=-float(BIG), in1=bank[4 + h][:], op0=ALU.mult, op1=ALU.add).then_inc(rank_step, 1)
            dve.wait_ge(rank_done, 3)
            dve.tensor_reduce(most[:], bank[6][:, 0:E], AX_X, ALU.max).then_inc(count_read, 1)
            dve.wait_ge(rank_step, 2)
            dve.tensor_scalar(int_a, rank_int[:], RA - 1, None, ALU.bitwise_and).then_inc(rank_step, 1)
            dve.wait_ge(count_read, 1)
            dve.tensor_copy(most_int[:], most[:]).then_inc(most_ready, 1)
            dve.wait_ge(rank_step, 3)
            dve.tensor_copy(rank_b[:].rearrange("p t e -> p (t e)"), int_a).then_inc(rank_step, 1)
            dve.wait_ge(rank_step, 4)
            dve.tensor_scalar(int_a, rank_int[:], RA.bit_length() - 1, None, ALU.arith_shift_right).then_inc(rank_step, 1)
            with dve.Fori(0, NT) as t:
                dve.tensor_tensor(hot_b[:, bass.ds(t, 1), :, :, :].rearrange("p o g b e -> p (o g) b e"),
                                  by_group(rank_b, t),
                                  iota_b[:].unsqueeze(1).broadcast_to([P, E // EG, RA, EG]), ALU.is_equal).then_inc(hot_b_ready, 1)
            dve.wait_ge(rank_step, 5)
            dve.tensor_copy(rank_a[:].rearrange("p t e -> p (t e)"), int_a).then_inc(rank_step, 1)
            dve.wait_ge(rank_step, 6)

            def hidden(i, n):
                dve.wait_ge(th_ready[i], n + 1)
                dve.wait_ge(y_done[i], n)
                dve.scalar_tensor_tensor(out=hid[i][:], in0=th[i][:], scalar=1.0, in1=bank[2 + i][:, 0:3 * P],
                                         op0=ALU.add, op1=ALU.mult).then_inc(hid_ready[i], 1)

            def y_evac(i, n):
                dve.wait_ge(y_done[i], n + 1)
                dve.wait_ge(y_stored[i], 16 * n)
                dve.tensor_copy(y_sb[i][:].rearrange("p s d -> p (s d)"), bank[4 + i][:]).then_inc(y_ready[i], 1)

            def finish(r, q, t):
                n = 6 * (NT * r + t)
                row = lambda a: a[:, bass.ds(t, 1), :].rearrange("p o e -> p (o e)")
                ranks = rank_int[:, bass.ds(t * E, E)]
                dve.wait_ge(exp_ready, GROUPS)
                dve.wait_ge(fin_step, n)
                dve.bn_stats(f_stats[:], row(xn_all))
                dve.scalar_tensor_tensor(out=f_w[:], in0=row(exp_all), scalar=1.0, in1=row(chosen),
                                         op0=ALU.mult, op1=ALU.mult, accum_out=f_sum[:])
                dve.tensor_scalar(f_slot[:], ranks, SLOTS - 1, None, ALU.bitwise_and)
                dve.tensor_scalar(f_q[:], ranks, SLOTS.bit_length() - 1, None, ALU.arith_shift_right).then_inc(fin_step, 1)
                dve.wait_ge(fin_step, n + 1)
                dve.reciprocal(f_inv[:], f_sum[:])
                dve.bn_aggr(f_mean_var[:], f_stats[:])
                dve.scalar_tensor_tensor(out=f_round_w[:], in0=f_q[:], scalar=round_q[:, bass.ds(q, 1)], in1=f_w[:],
                                         op0=ALU.is_equal, op1=ALU.mult)
                dve.scalar_tensor_tensor(out=f_k1[:], in0=row(chosen), scalar=ABOVE, in1=f_slot[:],
                                         op0=ALU.mult, op1=ALU.subtract).then_inc(fin_step, 1)
                dve.wait_ge(fin_step, n + 2)
                dve.tensor_tensor(f_key[:], f_k1[:], expert_row[:], ALU.subtract).then_inc(fin_step, 1)
                dve.wait_ge(fin_step, n + 3)
                dve.tensor_copy(row(mean_var2), f_mean_var[:])
                dve.max(f_top[:], f_key[:]).then_inc(fin_step, 1)
                dve.wait_ge(fin_step, n + 4)
                dve.tensor_scalar(row(y_row), f_top[:], -1.0, ABOVE, ALU.mult, ALU.add)
                for k in range(K):
                    ins = dve.scalar_tensor_tensor(out=f_hit[:, k, :], in0=f_key[:], scalar=f_top[:, k:k + 1], in1=f_round_w[:],
                                                   op0=ALU.is_equal, op1=ALU.mult, accum_out=f_wk[:, k:k + 1])
                ins.then_inc(fin_step, 1)
                dve.wait_ge(fin_step, n + 5)
                dve.tensor_scalar(row(weight)[:, 0:K], f_wk[:, 0:K], f_inv[:, 0:1], 0.5, ALU.mult, ALU.mult).then_inc(fin_step, 1)

            def one_round(r, q):
                dve.tensor_scalar(round_rank_a[:].rearrange("p t e -> p (t e)"), rank_a[:].rearrange("p t e -> p (t e)"),
                                  round_a[:, bass.ds(q, 1)], None, ALU.subtract).then_inc(own_step, 1)
                dve.wait_ge(own_step, 3 * r + 1)
                dve.sem_inc(hot_a_begun, 1)
                with dve.Fori(0, NT) as t:
                    dve.tensor_tensor(hot_a[:, bass.ds(t, 1), :, :, :].rearrange("p o g a e -> p (o g) a e"),
                                      by_group(round_rank_a, t),
                                      iota_a[:].unsqueeze(1).broadcast_to([P, E // EG, RA, EG]), ALU.is_equal).then_inc(hot_a_ready, 1)
                for h in range(2):
                    dve.wait_ge(hot_a_read, 2 * r + h + 1)
                    dve.tensor_tensor(own[:, h * 512:(h + 1) * 512].rearrange("p (g e) -> p g e", e=EG),
                                      bank[6 + h][:].rearrange("p (g e) -> p g e", e=EG),
                                      same_expert[:].unsqueeze(1).broadcast_to([P, 64, EG]), ALU.mult).then_inc(own_step, 1)
                dve.wait_ge(own_step, 3 * r + 3)
                dve.tensor_reduce(lists[:], own[:].rearrange("p (g e) -> p g e", e=EG), AX_X, ALU.add).then_inc(lists_ready, 1)
                dve.wait_ge(lists_t_done, r + 1)
                dve.tensor_copy(slot_token[:], bank[6][:, 0:2 * P].rearrange("p (h e) -> p h e", h=2)[:, :, 0:E]).then_inc(slots_ready, 1)

                n0 = r * (E // 2)
                hidden(0, n0)

                def four(t):
                    for u in range(2):
                        hidden(1, n0 + 2 * t + u)
                        y_evac(0, n0 + 2 * t + u)
                        if not (isinstance(t, int) and t == NT - 1 and u == 1):
                            hidden(0, n0 + 2 * t + u + 1)
                        y_evac(1, n0 + 2 * t + u)
                    finish(r, q, t)

                with dve.Fori(0, NT - 1) as t:
                    four(t)
                four(NT - 1)

            def add_extra(r):
                with dve.Fori(0, NT) as t:
                    total = extra[:, bass.ds(t, 1), :].rearrange("p o d -> p (o d)")
                    n = r * NT + t
                    dve.wait_ge(extra_in, K * 16 * (n + 1))
                    dve.wait_ge(extra_step, K * n)
                    dve.tensor_copy(wk_sb[:, 0:1, 0:K], weight[:, bass.ds(t, 1), 0:K]).then_inc(extra_step, 1)
                    for k in range(K):
                        dve.wait_ge(extra_step, K * n + k + 1)
                        dve.scalar_tensor_tensor(out=total, in0=yg[0][:, 0, k, :], scalar=wk_sb[:, 0, k:k + 1], in1=total,
                                                 op0=ALU.mult, op1=ALU.add).then_inc(extra_step if k < K - 1 else extra_done, 1)

            rounds(dve, one_round, add_extra)
            dve.memset(wk_sb[:], 0.0).then_inc(fin_done, 1)

            def z_of(b):
                dve.wait_ge(zt_done, b)
                for s in range(2):
                    t = 2 * b + s
                    ins = dve.tensor_scalar(z_sb[:, s, :], xn_all[:, bass.ds(t, 1), :].rearrange("p o d -> p (o d)"),
                                            mean_var2[:, bass.ds(t, 1), 0], rstd2[:, bass.ds(t, 1)],
                                            ALU.subtract, ALU.mult)
                ins.then_inc(z_ready, 1)

            def softmax_head(b):
                dve.wait_ge(scores_done, b + 1)
                dve.wait_ge(probs_ready, b)
                dve.tensor_tensor(scores, bank[3][:, 0:3 * P], causal[:], ALU.add).then_inc(scores_step, 1)
                dve.wait_ge(scores_step, 2 * b + 1)
                dve.tensor_reduce(row_max[:, 0:1], scores[:, 0:P], AX_X, ALU.max)
                dve.tensor_reduce(row_max[:, 1:2], scores[:, P:3 * P], AX_X, ALU.max).then_inc(scores_step, 1)
                dve.wait_ge(scores_step, 2 * b + 2)
                dve.tensor_scalar(row_bias[:], row_max[:], -SCALE, None, ALU.mult).then_inc(bias_ready, 1)

            def shared_hidden(b, i, m):
                c, w = (SC * i + m) % 2, SW[m]
                dve.wait_ge(tg_ready, SC * b + m + 1)
                if not isinstance(b, int) or SC * b + m >= 2:
                    dve.wait_ge(hs_ready, SC * b + m - 1)
                dve.scalar_tensor_tensor(out=hg[c][0:w, :], in0=tg[c][0:w, :], scalar=1.0, in1=bank[4 + c][0:w, 0:S],
                                         op0=ALU.add, op1=ALU.mult).then_inc(hg_step, 1)
                dve.wait_ge(hg_step, SC * b + m + 1)
                dve.wait_ge(down_done, b)
                dve.tensor_tensor(hs[0:w, m, :], hg[c][0:w, :], bank[4 + c][0:w, S:2 * S], ALU.mult).then_inc(hs_ready, 1)

            def combine(b, i, n, s):
                done = 2 * K * b + s * K + 1
                if s == 0:
                    dve.tensor_copy(wk_sb[:, :, 0:K], weight[:, bass.ds(2 * b, 2), 0:K]).then_inc(routed_step, 1)
                    dve.wait_ge(yg_in[i], 2 * K * 16 * (n + 1))
                    dve.wait_ge(routed_step, done)
                dve.scalar_tensor_tensor(out=routed[:, s, :], in0=yg[i][:, s, 0, :], scalar=wk_sb[:, s, 0:1],
                                         in1=extra[:, bass.ds(2 * b + s, 1), :].rearrange("p o d -> p (o d)"),
                                         op0=ALU.mult, op1=ALU.add).then_inc(routed_step, 1)
                for k in range(1, K):
                    dve.wait_ge(routed_step, done + k)
                    ins = dve.scalar_tensor_tensor(out=routed[:, s, :], in0=yg[i][:, s, k, :], scalar=wk_sb[:, s, k:k + 1],
                                                   in1=routed[:, s, :], op0=ALU.mult, op1=ALU.add)
                    ins.then_inc(yg_used[i] if (s, k) == (1, K - 1) else routed_step, 1)

            def add_shared(b, i, n):
                dve.wait_ge(yg_used[i], n + 1)
                dve.wait_ge(down_done, b + 1)
                dve.scalar_tensor_tensor(out=ffn, in0=bank[7][:], scalar=0.5, in1=routed.rearrange("p s d -> p (s d)"),
                                         op0=ALU.mult, op1=ALU.add).then_inc(ffn_ready, 1)

            def final(b, i, n):
                dve.wait_ge(pv_done, b + 1)
                for s in range(2):
                    ins = dve.scalar_tensor_tensor(out=att[:, s * H:(s + 1) * H], in0=bank[6][:, s * H:(s + 1) * H],
                                                   scalar=row_inv[:, s:s + 1],
                                                   in1=xn_all[:, bass.ds(2 * b + s, 1), :].rearrange("p o d -> p (o d)"),
                                                   op0=ALU.mult, op1=ALU.add)
                ins.then_inc(pv_read, 1)
                dve.wait_ge(ffn_th_ready, b + 1)
                dve.scalar_tensor_tensor(out=gated, in0=ffn_th, scalar=1.0, in1=ffn, op0=ALU.add, op1=ALU.mult).then_inc(final_step, 1)
                dve.wait_ge(pv_read, b + 1)
                dve.wait_ge(final_step, 2 * b + 1)
                dve.tensor_tensor(gated, gated, att, ALU.mult).then_inc(final_step, 1)
                dve.wait_ge(final_step, 2 * b + 2)
                dve.wait_ge(out_stored[i], 16 * n)
                dve.scalar_tensor_tensor(out=out_sb[i], in0=gated, scalar=0.5,
                                         in1=x_all[:, bass.ds(2 * b, 2), :].rearrange("p s d -> p (s d)"),
                                         op0=ALU.mult, op1=ALU.add).then_inc(out_ready[i], 1)

            def batch(b, i, n):
                first, last = (isinstance(b, int) and b == v for v in (0, NB - 1))
                pb, pi, pn = b - 1, 1 - i, n
                softmax_head(b)
                if not first:
                    combine(pb, pi, pn, 0)
                shared_hidden(b, i, 0)
                if not first:
                    combine(pb, pi, pn, 1)
                shared_hidden(b, i, 1)
                if not first:
                    add_shared(pb, pi, pn)
                if not last:
                    z_of(b + 1)
                shared_hidden(b, i, 2)
                if not first:
                    final(pb, pi, pn)
                dve.wait_ge(probs_ready, b + 1)
                dve.reciprocal(row_inv[:], row_sum[:]).then_inc(inv_ready, 1)
                dve.wait_ge(inv_ready, b + 1)

            dve.wait_ge(rstd2_ready, 1)
            z_of(0)
            batch(0, 0, 0)
            with dve.Fori(0, NB // 2 - 1) as j:
                batch(2 * j + 1, 1, j)
                batch(2 * j + 2, 0, j)
            batch(NB - 1, 1, NB // 2 - 1)
            combine(NB - 1, 1, NB // 2 - 1, 0)
            combine(NB - 1, 1, NB // 2 - 1, 1)
            add_shared(NB - 1, 1, NB // 2 - 1)
            final(NB - 1, 1, NB // 2 - 1)

        @block.tensor
        def _(pe):
            pe.wait_ge(qkv_in, 16)
            pe.wait_ge(o_in, 16)
            for w in range(2):
                left_w = qkv_sb[:, (0, 2)[w], :, :]
                right_w = (qkv_sb[:, 1, :, :], o_sb)[w]
                for m in range(HC):
                    for k in range(HC):
                        ins = pe.matmul(bank[6 + w][:, m * H:(m + 1) * H], left_w[:, k, m * P:(m + 1) * P],
                                        right_w[:, k, :], start=k == 0, stop=k == HC - 1)
                ins.then_inc(wqk_done, 1)

            pe.wait_ge(const_ready, 4)
            pe.wait_ge(gate_in, 16)
            for g in range(GROUPS):
                pe.wait_ge(xn_ready, g + 1)
                for u in range(2):
                    if g:
                        pe.wait_ge(xnt_ready, 2 * (g - 1) + u + 1)
                    for v in range(2):
                        for c in range(HC):
                            ins = pe.transpose(bank[u][:, c * 2 * P + v * P:c * 2 * P + (v + 1) * P],
                                               xn_all[:, g * GT + 2 * u + v, c * P:(c + 1) * P], ident[:])
                    ins.then_inc(xnt_done, 1)
                if g >= 2:
                    pe.wait_ge(logits_ready, g - 1)
                for i in range(GT):
                    t = g * GT + i
                    pe.wait_ge(xnt_ready, 2 * g + i // 2 + 1)
                    for c in range(HC):
                        ins = pe.matmul(bank[2 + g % 2][:, i * E:(i + 1) * E], xn_t[:, c, t * P:(t + 1) * P],
                                        gate_sb[:, c, :], start=c == 0, stop=c == HC - 1)
                ins.then_inc(logits_done, 1)
            for h in range(2):
                pe.wait_ge(chosen_ready, 2 * h + 2)
                pe.matmul(bank[4 + h][:], before[:], chosen[:, 8 * h:8 * h + 8, :].rearrange("p t e -> p (t e)"), start=True, stop=False)
                pe.wait_ge(before_step, 8 * h + 7)
                pe.matmul(bank[4 + h][:], ones[:], chosen_before[:, 8 * h:8 * h + 8, :].rearrange("p t e -> p (t e)"),
                          start=False, stop=True).then_inc(rank_done, 1)
            pe.wait_ge(wqk_ready, 2)
            pe.wait_ge(before_step, NT)
            pe.matmul(bank[6][:, 0:E], ones[:], chosen_before[:, NT, :], start=True, stop=True).then_inc(rank_done, 1)
            pe.wait_ge(count_read, 1)

            def product(t, first=False, last=False):
                for g in range(E // EG):
                    ins = pe.matmul(bank[6 + g // 4][:, (g % 4) * P:(g % 4 + 1) * P],
                                    hot_a[:, bass.ds(t, 1), g, :, :].rearrange("p o a e -> p (o a e)"),
                                    hot_b[:, bass.ds(t, 1), g, :, :].rearrange("p o b e -> p (o b e)"),
                                    start=first and g % 4 == 0, stop=last, skip_group_check=True)
                    if last and g % 4 == 3:
                        ins.then_inc(hot_a_read, 1)

            def transpose_x(i, n):
                pe.wait_ge(xg_in[i], 32 * (n + 1))
                pe.wait_ge(xg_t_ready[i], n)
                for h in range(2):
                    for c in range(HC):
                        ins = pe.transpose(bank[i][:, c * SLOTS + h * P:c * SLOTS + (h + 1) * P],
                                           xg[i][:, h, c * P:(c + 1) * P], ident[:])
                ins.then_inc(xg_t_done[i], 1)

            def up(i, n):
                pe.wait_ge(w1_in[i], 16 * (n + 1))
                pe.wait_ge(xg_t_ready[i], n + 1)
                pe.wait_ge(hid_ready[i], n)
                for c in range(HC):
                    pe.matmul(bank[2 + i][:, 0:SLOTS], w1_sb[i][:, c, 0:P], xg_t[i][:, c, :], start=c == 0, stop=c == HC - 1)
                for c in range(HC):
                    for h in range(2):
                        ins = pe.matmul(bank[2 + i][64 * h:64 * h + IR, SLOTS:SLOTS + P], w1_sb[i][:, c, P:I],
                                        xg_t[i][:, c, h * P:(h + 1) * P], start=c == 0, stop=c == HC - 1,
                                        skip_group_check=True)
                ins.then_inc(up_done[i], 1)

            def down(i, n):
                pe.wait_ge(w2_in[i], 48 * (n + 1))
                pe.wait_ge(hid_ready[i], n + 1)
                pe.wait_ge(y_ready[i], n)
                for h in range(2):
                    pe.matmul(bank[4 + i][:, h * H:(h + 1) * H], hid[i][:, h * P:(h + 1) * P], w2_sb[i][:], start=True, stop=False)
                    ins = pe.matmul(bank[4 + i][:, h * H:(h + 1) * H], hid[i][:, SLOTS:SLOTS + P], w2r_sb[i][:, h, :],
                                    start=False, stop=True)
                ins.then_inc(y_done[i], 1)

            def one_round(r, q):
                pe.wait_ge(hot_b_scaled, 1)
                pe.wait_ge(hot_a_ready, NT * r + 1)
                product(0, first=True)
                with pe.Fori(1, NT - 1) as t:
                    pe.wait_ge(hot_b_scaled, t + 1)
                    pe.wait_ge(hot_a_ready, NT * r + t + 1)
                    product(t)
                pe.wait_ge(hot_b_scaled, NT)
                pe.wait_ge(hot_a_ready, NT * r + NT)
                product(NT - 1, last=True)
                pe.wait_ge(lists_in, 16 * (E // EG) * (r + 1))
                for h in range(2):
                    ins = pe.transpose(bank[6][:, h * P:(h + 1) * P], lists_by_expert[:, h * P:(h + 1) * P], ident[:])
                ins.then_inc(lists_t_done, 1)

                n0 = r * (E // 2)
                transpose_x(0, n0)
                up(0, n0)
                transpose_x(1, n0)
                with pe.Fori(0, E // 2 - 1) as j:
                    up(1, n0 + j)
                    transpose_x(0, n0 + j + 1)
                    down(0, n0 + j)
                    up(0, n0 + j + 1)
                    transpose_x(1, n0 + j + 1)
                    down(1, n0 + j)
                n1 = n0 + E // 2 - 1
                up(1, n1)
                down(0, n1)
                down(1, n1)
                for i in range(2):
                    pe.wait_ge(xg_t_ready[i], n0 + E // 2)
                    pe.wait_ge(hid_ready[i], n0 + E // 2)
                    pe.wait_ge(y_ready[i], n0 + E // 2)

            rounds(pe, one_round)

            def transpose_z(b):
                pe.wait_ge(z_ready, b + 1)
                pe.wait_ge(pt_ready, b)
                for s in range(2):
                    for c in range(HC):
                        ins = pe.transpose(bank[0][:, c * S + s * P:c * S + (s + 1) * P], z_sb[:, s, c * P:(c + 1) * P], ident[:])
                ins.then_inc(zt_done, 1)

            def batch(b, i):
                pe.wait_ge(zt_ready, b + 1)
                pe.wait_ge(gt_ready, b)
                for m in range(HC):
                    for k in range(HC):
                        ins = pe.matmul(bank[1][:, m * S:(m + 1) * S], wqk[:, k, m * P:(m + 1) * P], z_t[:, k, :],
                                        start=k == 0, stop=k == HC - 1)
                ins.then_inc(gt_done, 1)
                pe.wait_ge(vo_ready, b)
                for s in range(2):
                    for k in range(HC):
                        ins = pe.matmul(bank[2][:, s * H:(s + 1) * H], z_t[:, k, s * P:(s + 1) * P], wvo[:, k, :],
                                        start=k == 0, stop=k == HC - 1)
                ins.then_inc(vo_done, 1)
                pe.wait_ge(gt_ready, b + 1)
                pe.wait_ge(bias_ready, b)
                for s in range(2):
                    cols = (slice(0, P), slice(P, 3 * P))[s]
                    for k in range(HC):
                        ins = pe.matmul(bank[3][:, cols], g_t[:, k, s * P:(s + 1) * P], z_t[:, k, 0:(s + 1) * P],
                                        start=k == 0, stop=k == HC - 1)
                ins.then_inc(scores_done, 1)
                for m in range(SC):
                    c = (SC * i + m) % 2
                    if not (isinstance(b, int) and b == 0 and m < 2):
                        pe.wait_ge(hs_ready, SC * b + m - 1)
                    for part in range(2):
                        for k in range(HC):
                            ins = pe.matmul(bank[4 + c][0:SW[m], part * S:(part + 1) * S],
                                            up_sb[:, k, part * SI + m * P:part * SI + m * P + SW[m]],
                                            xn_t[:, k, bass.ds(b * S, S)], start=k == 0, stop=k == HC - 1)
                    ins.then_inc(gu_done, 1)
                pe.wait_ge(probs_ready, b + 1)
                for m in range(3):
                    ins = pe.transpose(bank[0][:, m * P:(m + 1) * P], probs[:, m * P:(m + 1) * P], ident[:])
                ins.then_inc(pt_done, 1)
                pe.wait_ge(hs_ready, SC * (b + 1))
                pe.wait_ge(ffn_ready, b)
                for s in range(2):
                    for m in range(SC):
                        ins = pe.matmul(bank[7][:, s * H:(s + 1) * H], hs[0:SW[m], m, s * P:(s + 1) * P],
                                        down_sb[0:SW[m], m, :], start=m == 0, stop=m == SC - 1)
                ins.then_inc(down_done, 1)
                if not (isinstance(b, int) and b == NB - 1):
                    transpose_z(b + 1)
                pe.wait_ge(pt_ready, b + 1)
                pe.wait_ge(vo_ready, b + 1)
                pe.wait_ge(pv_read, b)
                pe.matmul(bank[6][:, 0:H], probs_t[:, 0:P], vo[:, 0, :], start=True, stop=True)
                pe.matmul(bank[6][:, H:2 * H], probs_t[:, P:2 * P], vo[:, 0, :], start=True, stop=False)
                pe.matmul(bank[6][:, H:2 * H], probs_t[:, 2 * P:3 * P], vo[:, 1, :], start=False, stop=True).then_inc(pv_done, 1)

            pe.wait_ge(wqk_ready, 2)
            pe.wait_ge(up_in, 16 * (1 + SC))
            transpose_z(0)
            batches(pe, batch)


def kernel(L0_attn_x, L0_attn_qkv, L0_attn_o_proj, L0_attn_gamma, L0_attn_beta, L0_ffn_gate_w,
           L0_ffn_experts_w1, L0_ffn_experts_w2, L0_ffn_shared_gate_up, L0_ffn_shared_down):
    import numpy as np
    import concourse.bacc as bacc
    from concourse.bass_utils import run_bass_kernel_spmd

    x = np.asarray(L0_attn_x)
    B, S, H = x.shape
    HC = H // P
    qkv = np.asarray(L0_attn_qkv)
    w1 = np.asarray(L0_ffn_experts_w1)
    w2 = np.asarray(L0_ffn_experts_w2)
    E, I, _ = w1.shape
    w2t = w2.transpose(0, 2, 1)
    up = np.asarray(L0_ffn_shared_gate_up)
    arrays = {
        "x_rows": x.reshape(B * S, H),
        "qkv_t": qkv.reshape(H, 3, HC, P).transpose(3, 1, 2, 0),
        "o_proj": np.asarray(L0_attn_o_proj),
        "gamma_beta": np.stack([np.asarray(L0_attn_gamma), np.asarray(L0_attn_beta)]).reshape(2, HC, P).transpose(2, 0, 1),
        "gate_t": np.asarray(L0_ffn_gate_w).reshape(E, HC, P).transpose(2, 1, 0),
        "w1_t": w1.reshape(E, I, HC, P).transpose(0, 3, 2, 1),
        "w2_main": w2t[:, 0:P, :],
        "w2_rest": w2t[:, P:I, :],
        "shared_up_t": up.reshape(-1, HC, P).transpose(2, 1, 0),
        "shared_down_t": np.asarray(L0_ffn_shared_down).T,
    }
    arrays = {f"in_{k}": np.ascontiguousarray(v) for k, v in arrays.items()}
    nc = bacc.Bacc("TRN2", target_bir_lowering=False, num_devices=1)
    args = [nc.dram_tensor(k, v.shape, mybir.dt.from_np(v.dtype), kind="ExternalInput").ap() for k, v in arrays.items()]
    out = nc.dram_tensor("out_rows", (B * S, H), F32, kind="ExternalOutput").ap()
    gated_moe_attention(nc, *args, out)
    r = run_bass_kernel_spmd(nc, [arrays], core_ids=[0])
    return r.results[0]["out_rows"].reshape(B, S, H)
```

```python
from contextlib import ExitStack

import concourse.bass as bass
from concourse import mybir

F32 = mybir.dt.float32
F16 = mybir.dt.float16
BF16 = mybir.dt.bfloat16
I32 = mybir.dt.int32
U32 = mybir.dt.uint32
ALU = mybir.AluOpType
ACT = mybir.ActivationFunctionType
AX_X = mybir.AxisListType.X

P = 128


def gated_moe_attention(nc, x, qkv_t, o_proj, gamma_beta, gate_t, w1_t, w2_main, w2_rest,
                        shared_up_t, shared_down_t, out):
    T, H = x.shape
    E, _, HC, I = w1_t.shape
    NT = T // P
    NB = 8
    S = T // NB
    K = 6
    SLOTS = 256
    ROUNDS = T // SLOTS
    IR = I - P
    SI = shared_down_t.shape[0]
    SC = (SI + P - 1) // P
    SW = [min(P, SI - m * P) for m in range(SC)]
    GROUPS, GT = 4, NT // 4
    RA = 16
    EG = 8
    BIG = 16384
    EPS = 1e-5
    SCALE = float(H) ** -0.5
    PAD, GONE = -1.0e38, -3.0e38
    ROUND_ROWS = E * SLOTS
    ABOVE = 4.0 * ROUND_ROWS

    xn_rows = nc.dram_tensor("xn_rows", [T, H], F32, kind="Internal").ap()
    y_rows = nc.dram_tensor("y_rows", [ROUND_ROWS, H], F32, kind="Internal").ap()

    with ExitStack() as ctx:
        def sb(name, shape, dt=F32):
            return ctx.enter_context(nc.sbuf_tensor(name, [P] + shape, dt))

        def sem(name):
            return ctx.enter_context(nc.semaphore(name))

        def sems(name):
            return [sem(f"{name}{i}") for i in range(2)]

        bank = [ctx.enter_context(nc.psum_tensor(f"bank{i}", [P, 512], F32)) for i in range(8)]

        ident = sb("ident", [P])
        before = sb("before", [P], BF16)
        ones = sb("ones", [P], BF16)
        iota_a = sb("iota_a", [RA, EG], F16)
        iota_b = sb("iota_b", [RA, EG], F16)
        token_no = sb("token_no", [NT])
        expert_row = sb("expert_row", [E], I32)
        same_expert = sb("same_expert", [EG])
        causal = sb("causal", [3 * P])
        minus_half = sb("minus_half", [NT])
        round_a = sb("round_a", [ROUNDS])
        round_q = sb("round_q", [ROUNDS])
        partition_e = sb("partition_e", [EG], F16)
        partition_a = sb("partition_a", [RA])
        select_a = sb("select_a", [RA, RA], F16)

        gb = sb("gb", [2, HC])
        gate_sb = sb("gate_sb", [HC, E])
        wqk = sb("wqk", [HC, H])
        wvo = sb("wvo", [HC, H])
        shared_sb = sb("shared_sb", [2 * HC * SI + SC * H])
        up_sb = shared_sb[:, 0:2 * HC * SI].rearrange("p (c i) -> p c i", c=HC)
        down_sb = shared_sb[:, 2 * HC * SI:].rearrange("p (m d) -> p m d", m=SC)
        qkv_sb = shared_sb[:, 0:3 * HC * H].rearrange("p (w c d) -> p w c d", w=3, c=HC)
        o_sb = shared_sb[:, 3 * HC * H:4 * HC * H].rearrange("p (c d) -> p c d", c=HC)

        x_all = sb("x_all", [NT, H])
        xn_all = sb("xn_all", [NT, H])
        xn_t = sb("xn_t", [HC, T])
        stats = sb("stats", [GT, 6])
        stats2 = sb("stats2", [NT, 6])
        mean_var = sb("mean_var", [NT, 2])
        rstd = sb("rstd", [NT])
        var_eps = sb("var_eps", [NT])

        logits = sb("logits", [NT, E + 2])
        left = sb("left", [GT, E + 2])
        top8 = sb("top8", [NT, 8])
        taken = sb("taken", [NT, 8])
        neg_max = sb("neg_max", [NT])
        exp_all = sb("exp_all", [NT, E])
        chosen = sb("chosen", [NT, E], BF16)
        chosen_before = sb("chosen_before", [NT + 1, E], BF16)
        most = sb("most", [1])
        most_int = sb("most_int", [1], I32)
        rank_int = sb("rank_int", [NT * E], I32)
        rank_a = sb("rank_a", [NT, E], F16)
        rank_b = sb("rank_b", [NT, E], F16)
        round_rank_a = sb("round_rank_a", [NT, E], F16)
        space_a = sb("space_a", [NT * RA * E // 2])
        space_b = sb("space_b", [NT * RA * E // 2])
        hot_a = space_a[:].bitcast(F16).rearrange("p (t g a e) -> p t g a e", t=NT, a=RA, e=EG)
        hot_b = space_b[:].bitcast(F16).rearrange("p (t g b e) -> p t g b e", t=NT, b=RA, e=EG)
        own = sb("own", [8 * P])
        int_a = own[:].bitcast(I32)
        lists = sb("lists", [P], F16)
        spread = own[:].bitcast(F16).rearrange("p (g a b) -> p g a b", g=E // EG, a=RA)
        slot_token = sb("slot_token", [2, E], U32)
        f_q = sb("f_q", [E], I32)
        f_slot = sb("f_slot", [E], I32)
        f_round_w = sb("f_round_w", [E])
        f_w = sb("f_w", [E])
        f_sum = sb("f_sum", [1])
        f_inv = sb("f_inv", [1])
        f_k1 = sb("f_k1", [E])
        f_key = sb("f_key", [E])
        f_top = sb("f_top", [8])
        f_hit = sb("f_hit", [K, E])
        f_wk = sb("f_wk", [8])
        weight = sb("weight", [NT, 8])
        y_row = sb("y_row", [NT, 8], U32)
        mean_var2 = sb("mean_var2", [NT, 2])
        rstd2 = sb("rstd2", [NT])
        minus_mean2 = sb("minus_mean2", [NT])
        shift2 = sb("shift2", [NT])

        extra = sb("extra", [NT, H])

        w1_sb = [sb(f"w1_sb{c}", [2, HC, I]) for c in range(2)]
        w2_sb = [sb(f"w2_sb{c}", [2, H]) for c in range(2)]
        w2r_sb = [sb(f"w2r_sb{c}", [2, 2, H]) for c in range(2)]
        idx_sb = [[sb(f"idx_sb{c}{i}", [2], U32) for i in range(2)] for c in range(2)]

        used = {0: 0, 1: 0}

        def room(which, n):
            space = (space_a, space_b)[which]
            start = used[which]
            used[which] = start + n
            assert used[which] <= NT * RA * E // 2
            return space[:, start:start + n]

        y_sb = [room(0, 4 * H).rearrange("p (i s d) -> p i s d", i=2, s=2) for _ in range(2)]
        xg = [[room(0, 2 * H).rearrange("p (s d) -> p s d", s=2) for _ in range(2)] for _ in range(2)]
        hid = [room(0, 3 * P) for _ in range(2)]
        th = [room(0, 3 * P) for _ in range(2)]
        xg_t = [room(0, HC * SLOTS).rearrange("p (c s) -> p c s", c=HC) for _ in range(2)]

        used[0] = 0
        yg = [room(0, 2 * K * H).rearrange("p (s k d) -> p s k d", s=2, k=K) for _ in range(2)]
        z_sb = room(0, 2 * H).rearrange("p (s d) -> p s d", s=2)
        z_t = room(0, HC * S).rearrange("p (c s) -> p c s", c=HC)
        g_t = room(0, HC * S).rearrange("p (c s) -> p c s", c=HC)
        vo = room(1, 2 * H).rearrange("p (s d) -> p s d", s=2)
        scores = room(1, 3 * P)
        probs = room(1, 3 * P)
        probs_t = room(1, 3 * P)
        tg = [room(1, S) for _ in range(2)]
        hg = [room(1, S) for _ in range(2)]
        hs = room(1, SC * S).rearrange("p (m s) -> p m s", m=SC)
        ffn = room(1, 2 * H).rearrange("p (s d) -> p s d", s=2)
        ffn_th = room(1, 2 * H)
        att = room(1, 2 * H)
        gated = room(1, 2 * H)
        out_sb = [room(1, 2 * H) for _ in range(2)]
        row_max = sb("row_max", [2])
        row_bias = sb("row_bias", [2])
        row_sum = sb("row_sum", [2])
        row_inv = sb("row_inv", [2])
        yi_sb = [sb(f"yi_sb{i}", [2, 8], U32) for i in range(2)]
        wk_sb = sb("wk_sb", [2, 8])

        x_in = [sem(f"x_in{g}") for g in range(GROUPS)]
        qkv_in, o_in, gb_in, gate_in, up_in = sem("qkv_in"), sem("o_in"), sem("gb_in"), sem("gate_in"), sem("up_in")
        pool_const, dve_const = sem("pool_const"), sem("dve_const")
        const_ready = sem("const_ready")
        wqk_done, wqk_ready = sem("wqk_done"), sem("wqk_ready")
        ln_step, var_ready, rstd_step, rstd_ready = sem("ln_step"), sem("var_ready"), sem("rstd_step"), sem("rstd_ready")
        xn_ready, xn_stored = sem("xn_ready"), sem("xn_stored")
        xnt_done, xnt_ready = sem("xnt_done"), sem("xnt_ready")
        logits_done, logits_ready, top_ready = sem("logits_done"), sem("logits_ready"), sem("top_ready")
        route_step, chosen_ready, exp_ready = sem("route_step"), sem("chosen_ready"), sem("exp_ready")
        before_step, rank_done, count_done = sem("before_step"), sem("rank_done"), sem("count_done")
        count_read, most_ready, rank_step, rank_ready = sem("count_read"), sem("most_ready"), sem("rank_step"), sem("rank_ready")
        hot_b_ready, hot_b_scaled, hot_a_ready, hot_a_read = sem("hot_b_ready"), sem("hot_b_scaled"), sem("hot_a_ready"), sem("hot_a_read")
        own_step, spread_ready, spread_done, slots_ready = (sem(n) for n in ("own_step", "spread_ready", "spread_done", "slots_ready"))
        idx_ready, xg_in = [sems("idx_ready0"), sems("idx_ready1")], [sems("xg_in0"), sems("xg_in1")]
        xg_t_done, xg_t_ready = [sems("xg_t_done0"), sems("xg_t_done1")], sems("xg_t_ready")
        w1_in, w2_in, w2r_clear = sems("w1_in"), sems("w2_in"), sem("w2r_clear")
        up_done, th_ready, hid_ready, y_done, y_ready, y_stored = (sems(n) for n in ("up_done", "th_ready", "hid_ready", "y_done", "y_ready", "y_stored"))
        fin_step, fin_done = sem("fin_step"), sem("fin_done")
        rounds_done, extra_idx_ready, extra_in, extra_step, extra_done = (
            sem(n) for n in ("rounds_done", "extra_idx_ready", "extra_in", "extra_step", "extra_done"))
        round_stored, extra_clear = sem("round_stored"), sem("extra_clear")
        gathers_begun, stores_begun, hot_a_begun = sem("gathers_begun"), sem("stores_begun"), sem("hot_a_begun")
        stats2_step, var2_ready, rstd2_step, shift2_ready = (sem(n) for n in ("stats2_step", "var2_ready", "rstd2_step", "shift2_ready"))
        yi_ready, yg_in, combined = sems("yi_ready"), sems("yg_in"), sems("combined")
        z_ready, zt_done, zt_ready = sem("z_ready"), sem("zt_done"), sem("zt_ready")
        gt_done, gt_ready, vo_done, vo_ready = sem("gt_done"), sem("gt_ready"), sem("vo_done"), sem("vo_ready")
        scores_done, scores_read, max_ready, bias_ready, probs_ready = (
            sem(n) for n in ("scores_done", "scores_read", "max_ready", "bias_ready", "probs_ready"))
        inv_ready, pt_done, pt_ready, pv_done, pv_read = sem("inv_ready"), sem("pt_done"), sem("pt_ready"), sem("pv_done"), sem("pv_read")
        gu_done, tg_ready, hg_step, hs_ready = sem("gu_done"), sem("tg_ready"), sem("hg_step"), sem("hs_ready")
        down_done, down_read, routed_step, ffn_th_ready = sem("down_done"), sem("down_read"), sem("routed_step"), sem("ffn_th_ready")
        final_step, out_ready, out_stored = sem("final_step"), sems("out_ready"), sems("out_stored")

        x_tiles = x.rearrange("(t p) d -> p t d", p=P)
        xn_tiles = xn_rows.rearrange("(t p) d -> p t d", p=P)
        out_tiles = out.rearrange("(t p) d -> p t d", p=P)

        block = ctx.enter_context(nc.Block())

        def rounds(eng, experts, again):
            experts(0)
            eng.wait_ge(most_ready, 1)
            n = eng.value_load(most_int[0:1, 0:1], min_val=1, max_val=T)
            with eng.If(n > SLOTS):
                with eng.Fori(1, ROUNDS) as r:
                    with eng.If(n > r * SLOTS):
                        again(r)

        def batches(body, eng):
            body(0, 0, 0)
            with eng.Fori(0, NB // 2 - 1) as j:
                body(2 * j + 1, 1, j)
                body(2 * j + 2, 0, j)
            body(NB - 1, 1, NB // 2 - 1)

        @block.sync
        def _(sp):
            for g in range(GROUPS):
                sp.dma_start(x_all[:, g * GT:(g + 1) * GT, :], x_tiles[:, g * GT:(g + 1) * GT, :]).then_inc(x_in[g], 16)
            def load_w1(p, c, np):
                for i in range(2):
                    sp.wait_ge(up_done[i], np)
                sp.dma_start(w1_sb[c][:], w1_t[bass.ds(2 * p, 2), :, :, :].rearrange("o p c i -> p o c i")).then_inc(w1_in[c], 16)

            def load_w2(p, c, np):
                for i in range(2):
                    sp.wait_ge(y_done[i], np)
                sp.dma_start(w2_sb[c][:], w2_main[bass.ds(2 * p, 2), :, :].rearrange("o p d -> p o d")).then_inc(w2_in[c], 16)
                rest = w2_rest[bass.ds(2 * p, 2), :, :].rearrange("o p d -> p o d")
                sp.dma_start(w2r_sb[c][0:IR, :, 0, :], rest).then_inc(w2_in[c], 16)
                sp.dma_start(w2r_sb[c][64:64 + IR, :, 1, :], rest).then_inc(w2_in[c], 16)

            def store_y(p, c, np):
                for i in range(2):
                    sp.wait_ge(y_ready[i], np)
                rows = y_rows[bass.ds(2 * p * SLOTS, 2 * SLOTS), :].rearrange("(o t p) d -> p o t d", o=2, p=P)
                sp.dma_start(rows, y_sb[c][:]).then_inc(y_stored[c], 16)

            def first_weights(r):
                sp.wait_ge(w2r_clear, 2)
                for c in range(2):
                    load_w1(c, c, r * (E // 2))
                    load_w2(c, c, r * (E // 2))

            def experts(r):
                n0 = r * (E // 2)
                with sp.Fori(0, E // 4 - 1) as j:
                    for c in range(2):
                        load_w1(2 * j + 2 + c, c, n0 + 2 * j + c + 1)
                        load_w2(2 * j + 2 + c, c, n0 + 2 * j + c + 1)
                        store_y(2 * j + c, c, n0 + 2 * j + c + 1)
                for c in range(2):
                    store_y(E // 2 - 2 + c, c, n0 + E // 2 - 1 + c)
                sp.wait_ge(xn_stored, 16 * GROUPS)
                for c in range(2):
                    sp.wait_ge(y_stored[c], 16 * (E // 4) * (r + 1))
                sp.sem_inc(round_stored, 1)

            def again(r):
                first_weights(r)
                sp.wait_ge(extra_done, NT * r)
                sp.sem_inc(stores_begun, 1)
                experts(r)

            for g in range(GROUPS):
                sp.wait_ge(xn_ready, g + 1)
                sp.dma_start(xn_tiles[:, g * GT:(g + 1) * GT, :], xn_all[:, g * GT:(g + 1) * GT, :]).then_inc(xn_stored, 16)
            first_weights(0)
            sp.wait_ge(wqk_done, 2)
            sp.dma_start(up_sb, shared_up_t).then_inc(up_in, 16)
            for m in range(SC):
                sp.dma_start(down_sb[0:SW[m], m, :], shared_down_t[m * P:m * P + SW[m], :]).then_inc(up_in, 16)
            rounds(sp, experts, again)
            sp.sem_inc(rounds_done, 1)

            with sp.Fori(0, NB // 2) as j:
                for i in range(2):
                    sp.wait_ge(out_ready[i], j + 1)
                    sp.dma_start(out_tiles[:, bass.ds(2 * (2 * j + i), 2), :],
                                 out_sb[i].rearrange("p (s d) -> p s d", s=2)).then_inc(out_stored[i], 16)
            for i in range(2):
                sp.wait_ge(out_stored[i], 16 * (NB // 2))
            sp.wait_ge(xn_stored, 16 * GROUPS)

        @block.gpsimd
        def _(pool):
            pool.memset(ident[:], 0.0).then_inc(pool_const, 1)
            pool.memset(ones[:], 1.0).then_inc(pool_const, 1)
            pool.memset(before[:], 1.0).then_inc(pool_const, 1)
            pool.memset(causal[:], 0.0).then_inc(pool_const, 1)
            pool.memset(minus_half[:], -0.5).then_inc(pool_const, 1)
            pool.memset(chosen_before[:, 0, :], 0.0).then_inc(pool_const, 1)
            pool.wait_ge(pool_const, 6)
            pool.affine_select(out=ident[:], in_=ident[:], compare_op=ALU.not_equal, fill=1.0, base=0,
                               pattern=[[-1, P]], channel_multiplier=1).then_inc(const_ready, 1)
            pool.affine_select(out=before[:], in_=before[:], compare_op=ALU.is_gt, fill=0.0, base=0,
                               pattern=[[1, P]], channel_multiplier=-1).then_inc(const_ready, 1)
            for m in (0, 2):
                pool.affine_select(out=causal[:, m * P:(m + 1) * P], in_=causal[:, m * P:(m + 1) * P],
                                   compare_op=ALU.is_ge, fill=-1.0e30, base=0,
                                   pattern=[[-1, P]], channel_multiplier=1).then_inc(const_ready, 1)

            pool.iota(int_a[:, 0:P], [[1, RA], [0, EG]], base=-(BIG // RA), channel_multiplier=0).then_inc(const_ready, 1)
            pool.iota(rank_int[:, 0:P], [[1, RA], [0, EG]], base=0, channel_multiplier=0).then_inc(const_ready, 1)
            pool.iota(int_a[:, P:P + NT], [[P, NT]], base=0, channel_multiplier=1).then_inc(const_ready, 1)
            pool.iota(int_a[:, 2 * P:2 * P + ROUNDS], [[SLOTS // RA, ROUNDS]], base=0, channel_multiplier=0).then_inc(const_ready, 1)
            pool.iota(int_a[:, 3 * P:3 * P + ROUNDS], [[1, ROUNDS]], base=-(BIG // SLOTS), channel_multiplier=0).then_inc(const_ready, 1)
            pool.iota(expert_row[:], [[SLOTS, E]], base=0, channel_multiplier=0).then_inc(const_ready, 1)

            def rstd_of(g):
                ts = slice(g * GT, (g + 1) * GT)
                pool.wait_ge(var_ready, g + 1)
                pool.tensor_scalar(var_eps[:, ts], mean_var[:, ts, 1], EPS, None, ALU.add).then_inc(rstd_step, 1)
                pool.wait_ge(rstd_step, g + 1)
                pool.tensor_tensor(rstd[:, ts], var_eps[:, ts], minus_half[:, ts], ALU.pow).then_inc(rstd_ready, 1)

            def count_before(g):
                pool.wait_ge(chosen_ready, g + 1)
                for t in range(g * GT, (g + 1) * GT):
                    if t:
                        pool.wait_ge(before_step, t)
                    pool.tensor_tensor(chosen_before[:, t + 1, :], chosen_before[:, t, :], chosen[:, t, :],
                                       ALU.add).then_inc(before_step, 1)

            rstd_of(0)
            rstd_of(1)
            rstd_of(2)
            count_before(0)
            rstd_of(3)
            for g in range(1, GROUPS):
                count_before(g)
            pool.memset(extra[:], 0.0).then_inc(extra_clear, 1)

            def gather_x(e, c, i, n):
                pool.wait_ge(xg_in[c][i], 32 * n)
                pool.tensor_copy(idx_sb[c][i][:], slot_token[:, :, bass.ds(e, 1)].rearrange("p h o -> p (h o)")).then_inc(idx_ready[c][i], 1)
                pool.wait_ge(idx_ready[c][i], n + 1)
                pool.wait_ge(xg_t_done[c][i], n)
                pool.sem_inc(gathers_begun, 1)
                for h in range(2):
                    pool.indirect_dma_start(xg[c][i][:, h, :], None, xn_rows,
                                            bass.IndirectOffsetOnAxis(ap=idx_sb[c][i][:, h:h + 1], axis=0)).then_inc(xg_in[c][i], 16)

            def experts(r):
                pool.wait_ge(xn_stored, 16 * GROUPS)
                pool.wait_ge(slots_ready, r + 1)
                pool.sem_inc(gathers_begun, 1)
                with pool.Fori(0, E // 4) as j:
                    for c in range(2):
                        for i in range(2):
                            gather_x(4 * j + 2 * c + i, c, i, r * (E // 4) + j)

            def gather_extra(r):
                with pool.Fori(0, NT) as t:
                    n = r * NT + t
                    pool.wait_ge(extra_in, K * 16 * n)
                    pool.tensor_copy(yi_sb[0][:, 0:1, :], y_row[:, bass.ds(t, 1), :]).then_inc(extra_idx_ready, 1)
                    pool.wait_ge(extra_idx_ready, n + 1)
                    pool.wait_ge(round_stored, r + 1)
                    pool.wait_ge(extra_done, n)
                    pool.sem_inc(gathers_begun, 1)
                    for k in range(K):
                        pool.indirect_dma_start(yg[0][:, 0, k, :], None, y_rows,
                                                bass.IndirectOffsetOnAxis(ap=yi_sb[0][:, 0, k:k + 1], axis=0)).then_inc(extra_in, 16)

            def again(r):
                gather_extra(r - 1)
                experts(r)

            rounds(pool, experts, again)

            pool.wait_ge(var2_ready, 1)
            pool.tensor_scalar(var_eps[:], mean_var2[:, :, 1], EPS, None, ALU.add).then_inc(rstd2_step, 1)
            pool.tensor_scalar(minus_mean2[:], mean_var2[:, :, 0], -1.0, None, ALU.mult).then_inc(rstd2_step, 1)
            pool.wait_ge(rstd2_step, 2)
            pool.tensor_tensor(rstd2[:], var_eps[:], minus_half[:], ALU.pow).then_inc(rstd2_step, 1)
            pool.wait_ge(rstd2_step, 3)
            pool.tensor_tensor(shift2[:], minus_mean2[:], rstd2[:], ALU.mult).then_inc(shift2_ready, 1)
            pool.wait_ge(fin_done, 1)
            pool.wait_ge(rounds_done, 1)
            with pool.Fori(0, NB // 2) as j:
                for i in range(2):
                    pool.wait_ge(yg_in[i], 2 * K * 16 * j)
                    pool.tensor_copy(yi_sb[i][:], y_row[:, bass.ds(2 * (2 * j + i), 2), :]).then_inc(yi_ready[i], 1)
                    pool.wait_ge(yi_ready[i], j + 1)
                    pool.wait_ge(combined[i], j)
                    pool.sem_inc(gathers_begun, 1)
                    for s in range(2):
                        for k in range(K):
                            pool.indirect_dma_start(yg[i][:, s, k, :], None, y_rows,
                                                    bass.IndirectOffsetOnAxis(ap=yi_sb[i][:, s, k:k + 1], axis=0)).then_inc(yg_in[i], 16)

        def exps(act, g):
            act.wait_ge(top_ready, g + 1)
            for t in range(g * GT, (g + 1) * GT):
                ins = act.activation(exp_all[:, t, :], logits[:, t, 0:E], ACT.Exp, bias=neg_max[:, t:t + 1])
            ins.then_inc(exp_ready, 1)

        @block.scalar
        def _(act):
            act.dma_start(gate_sb[:], gate_t).then_inc(gate_in, 16)
            act.dma_start(qkv_sb, qkv_t).then_inc(qkv_in, 16)
            act.dma_start(o_sb, o_proj.rearrange("(c p) n -> p c n", p=P)).then_inc(o_in, 16)
            act.dma_start(gb[:], gamma_beta).then_inc(gb_in, 16)

            def scale_b(t, n):
                act.wait_ge(hot_b_ready, n + 1)
                act.activation(hot_b[:, bass.ds(t, 1), :, :, :].rearrange("p o g b e -> p (o g b e)"),
                               hot_b[:, bass.ds(t, 1), :, :, :].rearrange("p o g b e -> p (o g b e)"), ACT.Copy,
                               scale=token_no[:, bass.ds(t, 1)]).then_inc(hot_b_scaled, 1)

            for g in range(GROUPS):
                for u in range(2):
                    act.wait_ge(xnt_done, 2 * g + u + 1)
                    t = g * GT + 2 * u
                    act.copy(xn_t[:, :, t * P:(t + 2) * P], bank[u][:].rearrange("p (c s) -> p c s", c=HC)).then_inc(xnt_ready, 1)
                if g:
                    exps(act, g - 1)
            for g in range(GROUPS):
                for t in range(g * GT, (g + 1) * GT):
                    scale_b(t, t)
            exps(act, GROUPS - 1)
            for w, dst in enumerate((wqk, wvo)):
                act.wait_ge(wqk_done, w + 1)
                act.copy(dst[:].rearrange("p c n -> p (c n)"), bank[w][:]).then_inc(wqk_ready, 1)

            def expert(c, i, n, m):
                act.wait_ge(xg_t_done[c][i], m + 1)
                act.wait_ge(up_done[i], n)
                act.copy(xg_t[i][:].rearrange("p c s -> p (c s)"), bank[i][:]).then_inc(xg_t_ready[i], 1)
                act.wait_ge(up_done[i], n + 1)
                act.wait_ge(hid_ready[i], n)
                act.activation(th[i][:], bank[2 + i][:, 0:3 * P], ACT.Tanh, scale=0.5).then_inc(th_ready[i], 1)

            def experts(r):
                with act.Fori(0, E // 4) as j:
                    for c in range(2):
                        for i in range(2):
                            expert(c, i, r * (E // 2) + 2 * j + c, r * (E // 4) + j)

            def again(r):
                with act.Fori(0, NT) as t:
                    scale_b(t, NT * r + t)
                experts(r)

            rounds(act, experts, again)

            def z_of(b):
                act.wait_ge(zt_done, b)
                for s in range(2):
                    t = 2 * b + s
                    ins = act.activation(z_sb[:, s, :], xn_all[:, bass.ds(t, 1), :].rearrange("p o d -> p (o d)"),
                                         ACT.Identity, bias=shift2[:, bass.ds(t, 1)], scale=rstd2[:, bass.ds(t, 1)])
                ins.then_inc(z_ready, 1)

            def z_evac(b):
                act.wait_ge(zt_done, b + 1)
                act.wait_ge(scores_done, b)
                for c in range(HC):
                    ins = act.activation(z_t[:, c, :], bank[3][:, c * S:(c + 1) * S], ACT.Identity,
                                         bias=gb[:, 1, c:c + 1], scale=gb[:, 0, c:c + 1])
                ins.then_inc(zt_ready, 1)

            def g_evac(b):
                act.wait_ge(gt_done, b + 1)
                act.copy(g_t.rearrange("p c s -> p (c s)"), bank[1][:]).then_inc(gt_ready, 1)

            def vo_evac(b):
                act.wait_ge(vo_done, b + 1)
                act.wait_ge(pv_done, b)
                act.copy(vo.rearrange("p s d -> p (s d)"), bank[2][:]).then_inc(vo_ready, 1)

            def gate_tanh(b, i, m):
                c = (SC * i + m) % 2
                act.wait_ge(gu_done, SC * b + m + 1)
                if not (isinstance(b, int) and b == 0 and m < 2):
                    act.wait_ge(hs_ready, SC * b + m - 1)
                act.activation(tg[c][0:SW[m], :], bank[4 + c][0:SW[m], 0:S], ACT.Tanh, scale=0.5).then_inc(tg_ready, 1)

            def ffn_tanh(b, i, n):
                act.wait_ge(combined[i], n + 1)
                act.activation(ffn_th, ffn.rearrange("p s d -> p (s d)"), ACT.Tanh, scale=0.5).then_inc(ffn_th_ready, 1)

            def batch(b, i, n):
                first, last = (isinstance(b, int) and b == v for v in (0, NB - 1))
                if not last:
                    z_of(b + 1)
                act.wait_ge(bias_ready, b + 1)
                act.wait_ge(pt_done, b)
                act.wait_ge(inv_ready, b)
                act.activation(probs[:, 0:P], scores[:, 0:P], ACT.Exp, bias=row_bias[:, 0:1], scale=SCALE,
                               accum_out=row_sum[:, 0:1])
                act.activation(probs[:, P:3 * P], scores[:, P:3 * P], ACT.Exp, bias=row_bias[:, 1:2], scale=SCALE,
                               accum_out=row_sum[:, 1:2]).then_inc(probs_ready, 1)
                gate_tanh(b, i, 0)
                gate_tanh(b, i, 1)
                if not last:
                    z_evac(b + 1)
                gate_tanh(b, i, 2)
                act.wait_ge(pt_done, b + 1)
                act.copy(probs_t, bank[0][:, 0:3 * P]).then_inc(pt_ready, 1)
                if not last:
                    g_evac(b + 1)
                if not first:
                    ffn_tanh(b - 1, 1 - i, n)
                if not last:
                    vo_evac(b + 1)

            act.wait_ge(gb_in, 16)
            act.wait_ge(shift2_ready, 1)
            z_of(0)
            z_evac(0)
            g_evac(0)
            vo_evac(0)
            batches(batch, act)
            ffn_tanh(NB - 1, 1, NB // 2 - 1)

        @block.vector
        def _(dve):
            dve.memset(logits[:, :, E:E + 2], PAD).then_inc(dve_const, 1)
            dve.memset(taken[:, :, K:8], PAD).then_inc(dve_const, 1)
            for i in range(2):
                dve.memset(w2r_sb[i][:], 0.0).then_inc(w2r_clear, 1)
                dve.memset(bank[2 + i][:], 0.0).then_inc(dve_const, 1)
            N_CONST = 4
            ln = [0]

            def statistics(g):
                dve.wait_ge(x_in[g], 16)
                for i in range(GT):
                    ins = dve.bn_stats(stats[:, i, :], x_all[:, g * GT + i, :])
                ins.then_inc(ln_step, 1)
                ln[0] += 1
                dve.wait_ge(ln_step, ln[0])
                for i in range(GT):
                    ins = dve.bn_aggr(mean_var[:, g * GT + i, :], stats[:, i, :])
                ins.then_inc(var_ready, 1)
                dve.wait_ge(var_ready, g + 1)

            def normalise(g):
                dve.wait_ge(rstd_ready, g + 1)
                for t in range(g * GT, (g + 1) * GT):
                    ins = dve.tensor_scalar(xn_all[:, t, :], x_all[:, t, :], mean_var[:, t, 0:1], rstd[:, t:t + 1],
                                            ALU.subtract, ALU.mult)
                ins.then_inc(xn_ready, 1)

            def by_group(ranks, t):
                return (ranks[:, bass.ds(t, 1), :].rearrange("p o (g e) -> p (o g) e", e=EG).unsqueeze(2)
                        .broadcast_to([P, E // EG, RA, EG]))

            rs = [0]

            def step(ins):
                rs[0] += 1
                ins.then_inc(route_step, 1)
                dve.wait_ge(route_step, rs[0])

            def route(g):
                ts = slice(g * GT, (g + 1) * GT)
                dve.wait_ge(logits_done, g + 1)
                dve.tensor_copy(logits[:, ts, 0:E], bank[2 + g % 2][:, 0:GT * E].rearrange("p (t e) -> p t e", e=E)).then_inc(logits_ready, 1)
                dve.wait_ge(logits_ready, g + 1)
                for t in range(g * GT, (g + 1) * GT):
                    ins = dve.max(top8[:, t, :], logits[:, t, 0:E])
                step(ins)
                dve.tensor_scalar(neg_max[:, ts], top8[:, ts, 0], -1.0, None, ALU.mult).then_inc(top_ready, 1)
                step(dve.tensor_copy(taken[:, ts, 0:K], top8[:, ts, 0:K]))
                for i in range(GT):
                    ins = dve.match_replace(left[:, i, :], taken[:, g * GT + i, :], logits[:, g * GT + i, :], GONE)
                step(ins)
                dve.tensor_tensor(chosen[:, ts, :], left[:, :, 0:E], logits[:, ts, 0:E], ALU.not_equal).then_inc(chosen_ready, 1)

            def rank(g):
                ts = slice(g * GT * E, (g + 1) * GT * E)
                flat = lambda a: a[:, g * GT:(g + 1) * GT, :].rearrange("p t e -> p (t e)")
                dve.wait_ge(rank_done, g + 1)
                dve.scalar_tensor_tensor(out=rank_int[:, ts], in0=flat(chosen), scalar=-float(BIG),
                                         in1=bank[4 + g // 2][:, (g % 2) * GT * E:(g % 2 + 1) * GT * E],
                                         op0=ALU.mult, op1=ALU.add).then_inc(rank_step, 1)
                dve.wait_ge(rank_step, 5 * g + 1)
                dve.tensor_scalar(int_a[:, ts], rank_int[:, ts], RA - 1, None, ALU.bitwise_and).then_inc(rank_step, 1)
                dve.wait_ge(rank_step, 5 * g + 2)
                dve.tensor_copy(flat(rank_b), int_a[:, ts]).then_inc(rank_step, 1)
                dve.wait_ge(rank_step, 5 * g + 3)
                dve.tensor_scalar(int_a[:, ts], rank_int[:, ts], RA.bit_length() - 1, None, ALU.arith_shift_right).then_inc(rank_step, 1)
                dve.wait_ge(rank_step, 5 * g + 4)
                dve.tensor_copy(flat(rank_a), int_a[:, ts]).then_inc(rank_step, 1)

            def one_hot(t, ranks_a):
                dve.tensor_tensor(hot_b[:, bass.ds(t, 1), :, :, :].rearrange("p o g b e -> p (o g) b e"), by_group(rank_b, t),
                                  iota_b[:].unsqueeze(1).broadcast_to([P, E // EG, RA, EG]), ALU.is_equal).then_inc(hot_b_ready, 1)
                dve.tensor_tensor(hot_a[:, bass.ds(t, 1), :, :, :].rearrange("p o g a e -> p (o g) a e"), by_group(ranks_a, t),
                                  iota_a[:].unsqueeze(1).broadcast_to([P, E // EG, RA, EG]), ALU.is_equal).then_inc(hot_a_ready, 1)

            def one_hots(g):
                dve.wait_ge(rank_step, 5 * g + 5)
                for t in range(g * GT, (g + 1) * GT):
                    one_hot(t, rank_a)

            dve.wait_ge(dve_const, N_CONST)
            statistics(0)
            dve.wait_ge(const_ready, 10)
            dve.tensor_copy(iota_a[:].rearrange("p a e -> p (a e)"), int_a[:, 0:P]).then_inc(dve_const, 1)
            dve.tensor_copy(iota_b[:].rearrange("p a e -> p (a e)"), rank_int[:, 0:P]).then_inc(dve_const, 1)
            dve.tensor_copy(token_no[:], int_a[:, P:P + NT]).then_inc(dve_const, 1)
            dve.tensor_copy(round_a[:], int_a[:, 2 * P:2 * P + ROUNDS]).then_inc(dve_const, 1)
            dve.tensor_copy(round_q[:], int_a[:, 3 * P:3 * P + ROUNDS]).then_inc(dve_const, 1)
            dve.tensor_reduce(same_expert[:], ident[:].rearrange("p (a e) -> p e a", a=RA), AX_X, ALU.add).then_inc(dve_const, 1)
            dve.tensor_reduce(partition_a[:], ident[:].rearrange("p (a e) -> p a e", a=RA), AX_X, ALU.add).then_inc(dve_const, 1)
            statistics(1)
            normalise(0)
            dve.wait_ge(dve_const, N_CONST + 7)
            dve.tensor_copy(partition_e[:], same_expert[:]).then_inc(dve_const, 1)
            dve.tensor_copy(select_a[:], partition_a[:].unsqueeze(2).broadcast_to([P, RA, RA])).then_inc(dve_const, 1)
            statistics(2)
            normalise(1)
            route(0)
            statistics(3)
            normalise(2)
            dve.wait_ge(dve_const, N_CONST + 9)
            rank(0)
            one_hots(0)
            route(1)
            normalise(3)
            rank(1)
            route(2)
            one_hots(1)
            rank(2)
            route(3)
            one_hots(2)
            rank(3)
            one_hots(3)

            def hidden(i, n):
                dve.wait_ge(th_ready[i], n + 1)
                dve.wait_ge(y_done[i], n)
                dve.scalar_tensor_tensor(out=hid[i][:], in0=th[i][:], scalar=1.0, in1=bank[2 + i][:, 0:3 * P],
                                         op0=ALU.add, op1=ALU.mult).then_inc(hid_ready[i], 1)

            def y_evac(c, i, n, m):
                dve.wait_ge(y_done[i], n + 1)
                dve.wait_ge(y_stored[c], 16 * m)
                dve.tensor_copy(y_sb[c][:, i, :, :].rearrange("p s d -> p (s d)"), bank[4 + i][:]).then_inc(y_ready[i], 1)

            def finish(r, t):
                n = 6 * (NT * r + t)
                row = lambda a: a[:, bass.ds(t, 1), :].rearrange("p o e -> p (o e)")
                ranks = rank_int[:, bass.ds(t * E, E)]
                dve.wait_ge(exp_ready, GROUPS)
                dve.wait_ge(fin_step, n)
                dve.scalar_tensor_tensor(out=f_w[:], in0=row(exp_all), scalar=1.0, in1=row(chosen),
                                         op0=ALU.mult, op1=ALU.mult, accum_out=f_sum[:])
                dve.tensor_scalar(f_slot[:], ranks, SLOTS - 1, None, ALU.bitwise_and)
                dve.tensor_scalar(f_q[:], ranks, SLOTS.bit_length() - 1, None, ALU.arith_shift_right).then_inc(fin_step, 1)
                dve.wait_ge(fin_step, n + 1)
                dve.reciprocal(f_inv[:], f_sum[:])
                dve.scalar_tensor_tensor(out=f_k1[:], in0=row(chosen), scalar=ABOVE, in1=f_slot[:],
                                         op0=ALU.mult, op1=ALU.subtract).then_inc(fin_step, 1)
                dve.wait_ge(fin_step, n + 2)
                dve.tensor_tensor(f_key[:], f_k1[:], expert_row[:], ALU.subtract).then_inc(fin_step, 1)
                dve.wait_ge(fin_step, n + 3)
                dve.scalar_tensor_tensor(out=f_round_w[:], in0=f_q[:], scalar=round_q[:, bass.ds(r, 1)], in1=f_w[:],
                                         op0=ALU.is_equal, op1=ALU.mult)
                dve.max(f_top[:], f_key[:]).then_inc(fin_step, 1)
                dve.wait_ge(fin_step, n + 4)
                dve.tensor_scalar(row(y_row), f_top[:], -1.0, ABOVE, ALU.mult, ALU.add)
                for k in range(K):
                    ins = dve.scalar_tensor_tensor(out=f_hit[:, k, :], in0=f_key[:], scalar=f_top[:, k:k + 1], in1=f_round_w[:],
                                                   op0=ALU.is_equal, op1=ALU.mult, accum_out=f_wk[:, k:k + 1])
                ins.then_inc(fin_step, 1)
                dve.wait_ge(fin_step, n + 5)
                dve.tensor_scalar(row(weight)[:, 0:K], f_wk[:, 0:K], f_inv[:, 0:1], 0.5, ALU.mult, ALU.mult).then_inc(fin_step, 1)

            def place_slots(r):
                n = 4 * r
                for h in range(2):
                    dve.wait_ge(hot_a_read, 2 * r + h + 1)
                    dve.tensor_tensor(own[:, h * 512:(h + 1) * 512].rearrange("p (g e) -> p g e", e=EG),
                                      bank[6 + h][:].rearrange("p (g e) -> p g e", e=EG),
                                      same_expert[:].unsqueeze(1).broadcast_to([P, 64, EG]), ALU.mult).then_inc(own_step, 1)
                dve.wait_ge(own_step, n + 2)
                with nc.allow_low_precision(reason="one number below 2048 among zeros"):
                    dve.tensor_reduce(lists[:], own[:].rearrange("p (g e) -> p g e", e=EG), AX_X, ALU.add).then_inc(own_step, 1)
                dve.wait_ge(own_step, n + 3)
                dve.tensor_tensor(spread, lists[:].rearrange("p (g b) -> p g b", g=E // EG).unsqueeze(2).broadcast_to([P, E // EG, RA, RA]),
                                  select_a[:].unsqueeze(1).broadcast_to([P, E // EG, RA, RA]), ALU.mult).then_inc(spread_ready, 1)
                dve.wait_ge(spread_done, r + 1)
                dve.tensor_copy(slot_token[:], bank[6][:, 0:2 * E].rearrange("p (h e) -> p h e", h=2)).then_inc(slots_ready, 1)

            def experts(r):
                n0, m0 = r * (E // 2), r * (E // 4)
                hidden(0, n0)

                def four(t):
                    for u in range(2):
                        hidden(1, n0 + 2 * t + u)
                        y_evac(u, 0, n0 + 2 * t + u, m0 + t)
                        if not (isinstance(t, int) and t == NT - 1 and u == 1):
                            hidden(0, n0 + 2 * t + u + 1)
                        y_evac(u, 1, n0 + 2 * t + u, m0 + t)
                    finish(r, t)

                def statistics2(t):
                    for u in range(2):
                        ins = dve.bn_stats(stats2[:, bass.ds(2 * t + u, 1), :].rearrange("p o d -> p (o d)"),
                                           xn_all[:, bass.ds(2 * t + u, 1), :].rearrange("p o d -> p (o d)"))
                    ins.then_inc(stats2_step, 1)

                if isinstance(r, int):
                    with dve.Fori(0, NT // 2) as t:
                        four(t)
                        statistics2(t)
                    dve.wait_ge(stats2_step, NT // 2)
                    for t in range(NT):
                        ins = dve.bn_aggr(mean_var2[:, t, :], stats2[:, t, :])
                    ins.then_inc(var2_ready, 1)
                    with dve.Fori(NT // 2, NT - 1) as t:
                        four(t)
                else:
                    with dve.Fori(0, NT - 1) as t:
                        four(t)
                four(NT - 1)

            def add_extra(r):
                with dve.Fori(0, NT) as t:
                    total = extra[:, bass.ds(t, 1), :].rearrange("p o d -> p (o d)")
                    n = r * NT + t
                    dve.wait_ge(extra_in, K * 16 * (n + 1))
                    dve.wait_ge(extra_step, K * n)
                    dve.tensor_copy(wk_sb[:, 0:1, 0:K], weight[:, bass.ds(t, 1), 0:K]).then_inc(extra_step, 1)
                    for k in range(K):
                        dve.wait_ge(extra_step, K * n + k + 1)
                        dve.scalar_tensor_tensor(out=total, in0=yg[0][:, 0, k, :], scalar=wk_sb[:, 0, k:k + 1], in1=total,
                                                 op0=ALU.mult, op1=ALU.add).then_inc(extra_step if k < K - 1 else extra_done, 1)

            def again(r):
                add_extra(r - 1)
                dve.tensor_scalar(round_rank_a[:].rearrange("p t e -> p (t e)"), rank_a[:].rearrange("p t e -> p (t e)"),
                                  round_a[:, bass.ds(r, 1)], None, ALU.subtract).then_inc(own_step, 1)
                dve.wait_ge(own_step, 4 * r)
                dve.sem_inc(hot_a_begun, 1)
                with dve.Fori(0, NT) as t:
                    one_hot(t, round_rank_a)
                place_slots(r)
                experts(r)

            place_slots(0)
            dve.wait_ge(extra_clear, 1)
            dve.wait_ge(count_done, 1)
            dve.tensor_reduce(most[:], bank[2][:, 0:E], AX_X, ALU.max).then_inc(count_read, 1)
            dve.wait_ge(count_read, 1)
            dve.tensor_copy(most_int[:], most[:]).then_inc(most_ready, 1)
            rounds(dve, experts, again)
            dve.memset(wk_sb[:], 0.0).then_inc(fin_done, 1)

            def softmax_head(b):
                dve.wait_ge(scores_done, b + 1)
                dve.wait_ge(probs_ready, b)
                dve.tensor_tensor(scores, bank[3][:, 0:3 * P], causal[:], ALU.add).then_inc(scores_read, 1)
                dve.wait_ge(scores_read, b + 1)
                dve.tensor_reduce(row_max[:, 0:1], scores[:, 0:P], AX_X, ALU.max)
                dve.tensor_reduce(row_max[:, 1:2], scores[:, P:3 * P], AX_X, ALU.max).then_inc(max_ready, 1)
                dve.wait_ge(max_ready, b + 1)
                dve.tensor_scalar(row_bias[:], row_max[:], -SCALE, None, ALU.mult).then_inc(bias_ready, 1)

            def shared_hidden(b, i, m):
                c, w = (SC * i + m) % 2, SW[m]
                dve.wait_ge(tg_ready, SC * b + m + 1)
                if not isinstance(b, int) or SC * b + m >= 2:
                    dve.wait_ge(hs_ready, SC * b + m - 1)
                dve.scalar_tensor_tensor(out=hg[c][0:w, :], in0=tg[c][0:w, :], scalar=1.0, in1=bank[4 + c][0:w, 0:S],
                                         op0=ALU.add, op1=ALU.mult).then_inc(hg_step, 1)
                dve.wait_ge(hg_step, SC * b + m + 1)
                dve.wait_ge(down_done, b)
                dve.tensor_tensor(hs[0:w, m, :], hg[c][0:w, :], bank[4 + c][0:w, S:2 * S], ALU.mult).then_inc(hs_ready, 1)

            def add_shared(b):
                dve.wait_ge(down_done, b + 1)
                dve.wait_ge(ffn_th_ready, b)
                dve.wait_ge(final_step, 2 * b)
                dve.scalar_tensor_tensor(out=ffn.rearrange("p s d -> p (s d)"), in0=bank[7][:], scalar=0.5,
                                         in1=extra[:, bass.ds(2 * b, 2), :].rearrange("p s d -> p (s d)"),
                                         op0=ALU.mult, op1=ALU.add).then_inc(down_read, 1)
                dve.tensor_copy(wk_sb[:, :, 0:K], weight[:, bass.ds(2 * b, 2), 0:K]).then_inc(routed_step, 1)

            def combine(b, i, n, rows):
                before = 2 * K * b
                for q in rows:
                    k, s = q // 2, q % 2
                    if q == 0:
                        dve.wait_ge(yg_in[i], 2 * K * 16 * (n + 1))
                        dve.wait_ge(down_read, b + 1)
                    dve.wait_ge(routed_step, before + max(q, 1))
                    dve.scalar_tensor_tensor(out=ffn[:, s, :], in0=yg[i][:, s, k, :], scalar=wk_sb[:, s, k:k + 1],
                                             in1=ffn[:, s, :], op0=ALU.mult, op1=ALU.add
                                             ).then_inc(combined[i] if q == 2 * K - 1 else routed_step, 1)

            def attended(b):
                dve.wait_ge(pv_done, b + 1)
                for s in range(2):
                    ins = dve.scalar_tensor_tensor(out=att[:, s * H:(s + 1) * H], in0=bank[6][:, s * H:(s + 1) * H],
                                                   scalar=row_inv[:, s:s + 1],
                                                   in1=xn_all[:, bass.ds(2 * b + s, 1), :].rearrange("p o d -> p (o d)"),
                                                   op0=ALU.mult, op1=ALU.add)
                ins.then_inc(pv_read, 1)

            def inverse(b):
                dve.wait_ge(probs_ready, b + 1)
                dve.wait_ge(pv_read, b)
                dve.reciprocal(row_inv[:], row_sum[:]).then_inc(inv_ready, 1)

            def final(b, i, n):
                dve.wait_ge(ffn_th_ready, b + 1)
                dve.scalar_tensor_tensor(out=gated, in0=ffn_th, scalar=1.0, in1=ffn.rearrange("p s d -> p (s d)"),
                                         op0=ALU.add, op1=ALU.mult).then_inc(final_step, 1)
                dve.wait_ge(pv_read, b + 1)
                dve.wait_ge(final_step, 2 * b + 1)
                dve.tensor_tensor(gated, gated, att, ALU.mult).then_inc(final_step, 1)
                dve.wait_ge(final_step, 2 * b + 2)
                dve.wait_ge(out_stored[i], 16 * n)
                dve.scalar_tensor_tensor(out=out_sb[i], in0=gated, scalar=0.5,
                                         in1=x_all[:, bass.ds(2 * b, 2), :].rearrange("p s d -> p (s d)"),
                                         op0=ALU.mult, op1=ALU.add).then_inc(out_ready[i], 1)

            def batch(b, i, n):
                first = isinstance(b, int) and b == 0
                pb, pi = b - 1, 1 - i
                softmax_head(b)
                if not first:
                    add_shared(pb)
                    combine(pb, pi, n, range(0, 2))
                shared_hidden(b, i, 0)
                if not first:
                    attended(pb)
                    combine(pb, pi, n, range(2, 4))
                shared_hidden(b, i, 1)
                if not first:
                    combine(pb, pi, n, range(4, 8))
                shared_hidden(b, i, 2)
                if not first:
                    combine(pb, pi, n, range(8, 2 * K))
                inverse(b)
                dve.wait_ge(inv_ready, b + 1)
                if not first:
                    final(pb, pi, n)

            batches(batch, dve)
            add_shared(NB - 1)
            combine(NB - 1, 1, NB // 2 - 1, range(2 * K))
            attended(NB - 1)
            final(NB - 1, 1, NB // 2 - 1)

        @block.tensor
        def _(pe):
            def product(t, first=False, last=False):
                for g in range(E // EG):
                    ins = pe.matmul(bank[6 + g // 4][:, (g % 4) * P:(g % 4 + 1) * P],
                                    hot_a[:, bass.ds(t, 1), g, :, :].rearrange("p o a e -> p (o a e)"),
                                    hot_b[:, bass.ds(t, 1), g, :, :].rearrange("p o b e -> p (o b e)"),
                                    start=first and g % 4 == 0, stop=last, skip_group_check=True)
                    if last and g % 4 == 3:
                        ins.then_inc(hot_a_read, 1)

            def rank(g):
                dst = bank[4 + g // 2][:, (g % 2) * GT * E:(g % 2 + 1) * GT * E]
                pe.wait_ge(chosen_ready, g + 1)
                pe.matmul(dst, before[:], chosen[:, g * GT:(g + 1) * GT, :].rearrange("p t e -> p (t e)"), start=True, stop=False)
                pe.wait_ge(before_step, (g + 1) * GT - 1)
                pe.matmul(dst, ones[:], chosen_before[:, g * GT:(g + 1) * GT, :].rearrange("p t e -> p (t e)"),
                          start=False, stop=True).then_inc(rank_done, 1)

            def products(g):
                for t in range(g * GT, (g + 1) * GT):
                    pe.wait_ge(hot_b_scaled, t + 1)
                    pe.wait_ge(hot_a_ready, t + 1)
                    product(t, first=t == 0, last=t == NT - 1)

            pe.wait_ge(const_ready, 4)
            pe.wait_ge(gate_in, 16)
            def logits_of(g):
                pe.wait_ge(xn_ready, g + 1)
                for u in range(2):
                    if g:
                        pe.wait_ge(xnt_ready, 2 * (g - 1) + u + 1)
                    for v in range(2):
                        for c in range(HC):
                            ins = pe.transpose(bank[u][:, c * 2 * P + v * P:c * 2 * P + (v + 1) * P],
                                               xn_all[:, g * GT + 2 * u + v, c * P:(c + 1) * P], ident[:])
                    ins.then_inc(xnt_done, 1)
                if g >= 2:
                    pe.wait_ge(logits_ready, g - 1)
                for i in range(GT):
                    t = g * GT + i
                    pe.wait_ge(xnt_ready, 2 * g + i // 2 + 1)
                    for c in range(HC):
                        ins = pe.matmul(bank[2 + g % 2][:, i * E:(i + 1) * E], xn_t[:, c, t * P:(t + 1) * P],
                                        gate_sb[:, c, :], start=c == 0, stop=c == HC - 1)
                ins.then_inc(logits_done, 1)

            logits_of(0)
            logits_of(1)
            rank(0)
            logits_of(2)
            rank(1)
            logits_of(3)
            products(0)
            rank(2)
            products(1)
            rank(3)
            products(2)
            products(3)
            def place_slots(r):
                pe.wait_ge(spread_ready, r + 1)
                for h in range(2):
                    for g in range(E // EG):
                        ins = pe.matmul(bank[6][:, h * E + g * EG:h * E + (g + 1) * EG],
                                        spread[:, g, h * RA // 2:(h + 1) * RA // 2, :].rearrange("p a b -> p (a b)"),
                                        partition_e[:], start=True, stop=True)
                ins.then_inc(spread_done, 1)

            def transpose_x(c, i, n, m):
                pe.wait_ge(xg_in[c][i], 32 * (m + 1))
                pe.wait_ge(xg_t_ready[i], n)
                for h in range(2):
                    for k in range(HC):
                        ins = pe.transpose(bank[i][:, k * SLOTS + h * P:k * SLOTS + (h + 1) * P],
                                           xg[c][i][:, h, k * P:(k + 1) * P], ident[:])
                ins.then_inc(xg_t_done[c][i], 1)

            def up(c, i, n, m):
                pe.wait_ge(w1_in[c], 16 * (m + 1))
                pe.wait_ge(xg_t_ready[i], n + 1)
                pe.wait_ge(hid_ready[i], n)
                for k in range(HC):
                    pe.matmul(bank[2 + i][:, 0:SLOTS], w1_sb[c][:, i, k, 0:P], xg_t[i][:, k, :], start=k == 0, stop=k == HC - 1)
                for k in range(HC):
                    for h in range(2):
                        ins = pe.matmul(bank[2 + i][64 * h:64 * h + IR, SLOTS:SLOTS + P], w1_sb[c][:, i, k, P:I],
                                        xg_t[i][:, k, h * P:(h + 1) * P], start=k == 0, stop=k == HC - 1,
                                        skip_group_check=True)
                ins.then_inc(up_done[i], 1)

            def down(c, i, n, m):
                pe.wait_ge(w2_in[c], 48 * (m + 1))
                pe.wait_ge(hid_ready[i], n + 1)
                pe.wait_ge(y_ready[i], n)
                for h in range(2):
                    pe.matmul(bank[4 + i][:, h * H:(h + 1) * H], hid[i][:, h * P:(h + 1) * P], w2_sb[c][:, i, :], start=True, stop=False)
                    ins = pe.matmul(bank[4 + i][:, h * H:(h + 1) * H], hid[i][:, SLOTS:SLOTS + P], w2r_sb[c][:, i, h, :],
                                    start=False, stop=True)
                ins.then_inc(y_done[i], 1)

            def experts(r):
                n0, m0 = r * (E // 2), r * (E // 4)

                def steps(j, c, last=False):
                    n, m = n0 + 2 * j + c, m0 + j
                    d, m_next = 1 - c, m0 + j + c
                    up(c, 1, n, m)
                    if not last:
                        transpose_x(d, 0, n + 1, m_next)
                    down(c, 0, n, m)
                    if not last:
                        up(d, 0, n + 1, m_next)
                        transpose_x(d, 1, n + 1, m_next)
                    down(c, 1, n, m)

                transpose_x(0, 0, n0, m0)
                up(0, 0, n0, m0)
                transpose_x(0, 1, n0, m0)
                with pe.Fori(0, E // 4 - 1) as j:
                    steps(j, 0)
                    steps(j, 1)
                steps(E // 4 - 1, 0)
                steps(E // 4 - 1, 1, last=True)
                for i in range(2):
                    pe.wait_ge(xg_t_ready[i], n0 + E // 2)
                    pe.wait_ge(hid_ready[i], n0 + E // 2)
                    pe.wait_ge(y_ready[i], n0 + E // 2)

            def again(r):
                pe.wait_ge(hot_b_scaled, NT * r + 1)
                pe.wait_ge(hot_a_ready, NT * r + 1)
                product(0, first=True)
                with pe.Fori(1, NT - 1) as t:
                    pe.wait_ge(hot_b_scaled, NT * r + t + 1)
                    pe.wait_ge(hot_a_ready, NT * r + t + 1)
                    product(t)
                pe.wait_ge(hot_b_scaled, NT * (r + 1))
                pe.wait_ge(hot_a_ready, NT * (r + 1))
                product(NT - 1, last=True)
                place_slots(r)
                experts(r)

            pe.wait_ge(before_step, NT)
            pe.wait_ge(logits_ready, GROUPS)
            pe.matmul(bank[2][:, 0:E], ones[:], chosen_before[:, NT, :], start=True, stop=True).then_inc(count_done, 1)

            pe.wait_ge(qkv_in, 16)
            pe.wait_ge(o_in, 16)
            pe.wait_ge(xnt_ready, 2 * GROUPS)

            def weights_product(w):
                left_w = qkv_sb[:, (0, 2)[w], :, :]
                right_w = (qkv_sb[:, 1, :, :], o_sb)[w]
                for m in range(HC):
                    for k in range(HC):
                        ins = pe.matmul(bank[w][:, m * H:(m + 1) * H], left_w[:, k, m * P:(m + 1) * P],
                                        right_w[:, k, :], start=k == 0, stop=k == HC - 1)
                ins.then_inc(wqk_done, 1)

            weights_product(0)
            place_slots(0)
            weights_product(1)
            pe.wait_ge(wqk_ready, 2)
            pe.wait_ge(count_read, 1)
            rounds(pe, experts, again)

            def transpose_z(b):
                pe.wait_ge(z_ready, b + 1)
                pe.wait_ge(scores_read, b)
                for s in range(2):
                    for c in range(HC):
                        ins = pe.transpose(bank[3][:, c * S + s * P:c * S + (s + 1) * P], z_sb[:, s, c * P:(c + 1) * P], ident[:])
                ins.then_inc(zt_done, 1)

            def g_of(b):
                pe.wait_ge(zt_ready, b + 1)
                pe.wait_ge(gt_ready, b)
                for m in range(HC):
                    for k in range(HC):
                        ins = pe.matmul(bank[1][:, m * S:(m + 1) * S], wqk[:, k, m * P:(m + 1) * P], z_t[:, k, :],
                                        start=k == 0, stop=k == HC - 1)
                ins.then_inc(gt_done, 1)

            def vo_of(b):
                pe.wait_ge(vo_ready, b)
                for s in range(2):
                    for k in range(HC):
                        ins = pe.matmul(bank[2][:, s * H:(s + 1) * H], z_t[:, k, s * P:(s + 1) * P], wvo[:, k, :],
                                        start=k == 0, stop=k == HC - 1)
                ins.then_inc(vo_done, 1)

            def scores_of(b):
                pe.wait_ge(gt_ready, b + 1)
                for s in range(2):
                    cols = (slice(0, P), slice(P, 3 * P))[s]
                    for k in range(HC):
                        ins = pe.matmul(bank[3][:, cols], g_t[:, k, s * P:(s + 1) * P], z_t[:, k, 0:(s + 1) * P],
                                        start=k == 0, stop=k == HC - 1)
                ins.then_inc(scores_done, 1)

            def gate_up(b, i, m):
                c = (SC * i + m) % 2
                if not (isinstance(b, int) and b == 0 and m < 2):
                    pe.wait_ge(hs_ready, SC * b + m - 1)
                for part in range(2):
                    for k in range(HC):
                        ins = pe.matmul(bank[4 + c][0:SW[m], part * S:(part + 1) * S],
                                        up_sb[:, k, part * SI + m * P:part * SI + m * P + SW[m]],
                                        xn_t[:, k, bass.ds(b * S, S)], start=k == 0, stop=k == HC - 1)
                ins.then_inc(gu_done, 1)

            def batch(b, i, n):
                last = isinstance(b, int) and b == NB - 1
                gate_up(b, i, 0)
                gate_up(b, i, 1)
                if not last:
                    transpose_z(b + 1)
                gate_up(b, i, 2)
                pe.wait_ge(probs_ready, b + 1)
                pe.wait_ge(pt_ready, b)
                for m in range(3):
                    ins = pe.transpose(bank[0][:, m * P:(m + 1) * P], probs[:, m * P:(m + 1) * P], ident[:])
                ins.then_inc(pt_done, 1)
                if not last:
                    g_of(b + 1)
                pe.wait_ge(pt_ready, b + 1)
                pe.wait_ge(vo_ready, b + 1)
                pe.wait_ge(pv_read, b)
                pe.matmul(bank[6][:, 0:H], probs_t[:, 0:P], vo[:, 0, :], start=True, stop=True)
                pe.matmul(bank[6][:, H:2 * H], probs_t[:, P:2 * P], vo[:, 0, :], start=True, stop=False)
                pe.matmul(bank[6][:, H:2 * H], probs_t[:, 2 * P:3 * P], vo[:, 1, :], start=False, stop=True).then_inc(pv_done, 1)
                pe.wait_ge(hs_ready, SC * (b + 1))
                pe.wait_ge(down_read, b)
                for s in range(2):
                    for m in range(SC):
                        ins = pe.matmul(bank[7][:, s * H:(s + 1) * H], hs[0:SW[m], m, s * P:(s + 1) * P],
                                        down_sb[0:SW[m], m, :], start=m == 0, stop=m == SC - 1)
                ins.then_inc(down_done, 1)
                if not last:
                    vo_of(b + 1)
                    scores_of(b + 1)

            pe.wait_ge(up_in, 16 * (1 + SC))
            transpose_z(0)
            g_of(0)
            vo_of(0)
            scores_of(0)
            batches(batch, pe)


def kernel(L0_attn_x, L0_attn_qkv, L0_attn_o_proj, L0_attn_gamma, L0_attn_beta, L0_ffn_gate_w,
           L0_ffn_experts_w1, L0_ffn_experts_w2, L0_ffn_shared_gate_up, L0_ffn_shared_down):
    import numpy as np
    import concourse.bacc as bacc
    from concourse.bass_utils import run_bass_kernel_spmd

    x = np.asarray(L0_attn_x)
    B, S, H = x.shape
    HC = H // P
    qkv = np.asarray(L0_attn_qkv)
    w1 = np.asarray(L0_ffn_experts_w1)
    w2 = np.asarray(L0_ffn_experts_w2)
    E, I, _ = w1.shape
    w2t = w2.transpose(0, 2, 1)
    up = np.asarray(L0_ffn_shared_gate_up)
    arrays = {
        "x_rows": x.reshape(B * S, H),
        "qkv_t": qkv.reshape(H, 3, HC, P).transpose(3, 1, 2, 0),
        "o_proj": np.asarray(L0_attn_o_proj),
        "gamma_beta": np.stack([np.asarray(L0_attn_gamma), np.asarray(L0_attn_beta)]).reshape(2, HC, P).transpose(2, 0, 1),
        "gate_t": np.asarray(L0_ffn_gate_w).reshape(E, HC, P).transpose(2, 1, 0),
        "w1_t": w1.reshape(E, I, HC, P).transpose(0, 3, 2, 1),
        "w2_main": w2t[:, 0:P, :],
        "w2_rest": w2t[:, P:I, :],
        "shared_up_t": up.reshape(-1, HC, P).transpose(2, 1, 0),
        "shared_down_t": np.asarray(L0_ffn_shared_down).T,
    }
    arrays = {f"in_{k}": np.ascontiguousarray(v) for k, v in arrays.items()}
    nc = bacc.Bacc("TRN2", target_bir_lowering=False, num_devices=1)
    args = [nc.dram_tensor(k, v.shape, mybir.dt.from_np(v.dtype), kind="ExternalInput").ap() for k, v in arrays.items()]
    out = nc.dram_tensor("out_rows", (B * S, H), F32, kind="ExternalOutput").ap()
    gated_moe_attention(nc, *args, out)
    r = run_bass_kernel_spmd(nc, [arrays], core_ids=[0])
    return r.results[0]["out_rows"].reshape(B, S, H)
```

```python
from contextlib import ExitStack

import concourse.bass as bass
from concourse import mybir

F32 = mybir.dt.float32
F16 = mybir.dt.float16
BF16 = mybir.dt.bfloat16
I32 = mybir.dt.int32
U32 = mybir.dt.uint32
ALU = mybir.AluOpType
ACT = mybir.ActivationFunctionType
AX_X = mybir.AxisListType.X

P = 128


def gated_moe_attention(nc, x, qkv_t, o_proj, gamma_beta, gate_t, w1_t, w2_main, w2_rest,
                        shared_up_t, shared_down_t, out):
    T, H = x.shape
    E, _, HC, I = w1_t.shape
    NT = T // P
    NB = 8
    S = T // NB
    K = 6
    SLOTS = 256
    ROUNDS = T // SLOTS
    IR = I - P
    SI = shared_down_t.shape[0]
    SC = (SI + P - 1) // P
    SW = [min(P, SI - m * P) for m in range(SC)]
    LATE = 4
    GROUPS, GT = 4, NT // 4
    AHEAD = 6
    RA = 16
    EG = 8
    BIG = 16384
    EPS = 1e-5
    SCALE = float(H) ** -0.5
    PAD, GONE = -1.0e38, -3.0e38
    ROUND_ROWS = E * SLOTS
    ABOVE = 4.0 * ROUND_ROWS

    xn_rows = nc.dram_tensor("xn_rows", [T, H], F32, kind="Internal").ap()
    y_rows = nc.dram_tensor("y_rows", [ROUND_ROWS, H], F32, kind="Internal").ap()

    with ExitStack() as ctx:
        def sb(name, shape, dt=F32):
            return ctx.enter_context(nc.sbuf_tensor(name, [P] + shape, dt))

        def sem(name):
            return ctx.enter_context(nc.semaphore(name))

        def sems(name):
            return [sem(f"{name}{i}") for i in range(2)]

        bank = [ctx.enter_context(nc.psum_tensor(f"bank{i}", [P, 512], F32)) for i in range(8)]

        ident = sb("ident", [P])
        before = sb("before", [P], BF16)
        ones = sb("ones", [P], BF16)
        iota_a = sb("iota_a", [RA, EG], F16)
        iota_b = sb("iota_b", [RA, EG], F16)
        token_no = sb("token_no", [NT])
        expert_row = sb("expert_row", [E], I32)
        same_expert = sb("same_expert", [EG])
        causal = sb("causal", [3 * P])
        minus_half = sb("minus_half", [NT])
        round_a = sb("round_a", [ROUNDS])
        round_q = sb("round_q", [ROUNDS])
        partition_e = sb("partition_e", [EG], F16)
        partition_a = sb("partition_a", [RA])
        select_a = sb("select_a", [RA, RA], F16)

        gb = sb("gb", [2, HC])
        gate_sb = sb("gate_sb", [HC, E])
        wqk = sb("wqk", [HC, H])
        wvo = sb("wvo", [HC, H])
        up_sb = sb("up_sb", [HC, 2 * SI])
        down_sb = sb("down_sb", [SC, H])
        tg = [sb(f"tg{c}", [S]) for c in range(2)]
        hg = [sb(f"hg{c}", [S]) for c in range(2)]
        hs = sb("hs", [SC, S])

        x_all = sb("x_all", [NT, H])
        xn_all = sb("xn_all", [NT, H])
        xn_t = sb("xn_t", [HC, T])
        stats = sb("stats", [GT, 6])
        stats2 = sb("stats2", [NT, 6])
        mean_var = sb("mean_var", [NT, 2])
        rstd = sb("rstd", [NT])
        var_eps = sb("var_eps", [NT])
        minus_mean = sb("minus_mean", [NT])
        shift = sb("shift", [NT])

        logits = sb("logits", [NT, E + 2])
        left = sb("left", [GT, E + 2])
        top8 = sb("top8", [NT, 8])
        taken = sb("taken", [NT, 8])
        neg_max = sb("neg_max", [NT])
        exp_all = sb("exp_all", [NT, E])
        chosen = sb("chosen", [NT, E], BF16)
        chosen_before = sb("chosen_before", [NT + 1, E], BF16)
        most = sb("most", [1])
        most_int = sb("most_int", [1], I32)
        rank_int = sb("rank_int", [NT * E], I32)
        rank_a = sb("rank_a", [NT, E], F16)
        rank_b = sb("rank_b", [NT, E], F16)
        round_rank_a = sb("round_rank_a", [NT, E], F16)
        space_a = sb("space_a", [NT * RA * E // 2])
        space_b = sb("space_b", [NT * RA * E // 2])
        hot_a = space_a[:].bitcast(F16).rearrange("p (t g a e) -> p t g a e", t=NT, a=RA, e=EG)
        hot_b = space_b[:].bitcast(F16).rearrange("p (t g b e) -> p t g b e", t=NT, b=RA, e=EG)
        own = sb("own", [8 * P])
        int_a = own[:].bitcast(I32)
        lists = sb("lists", [P], F16)
        spread = own[:].bitcast(F16).rearrange("p (g a b) -> p g a b", g=E // EG, a=RA)
        slot_token = sb("slot_token", [2, E], U32)
        f_q = sb("f_q", [E], I32)
        f_slot = sb("f_slot", [E], I32)
        f_round_w = sb("f_round_w", [E])
        f_w = sb("f_w", [E])
        f_sum = sb("f_sum", [1])
        f_inv = sb("f_inv", [1])
        f_k1 = sb("f_k1", [E])
        f_key = sb("f_key", [E])
        f_top = sb("f_top", [8])
        f_hit = sb("f_hit", [K, E])
        f_wk = sb("f_wk", [8])
        weight = sb("weight", [NT, 8])
        y_row = sb("y_row", [NT, 8], U32)
        mean_var2 = sb("mean_var2", [NT, 2])
        rstd2 = sb("rstd2", [NT])
        shift2 = sb("shift2", [NT])

        extra = sb("extra", [NT, H])
        qkv_sb = extra[:, 2:2 + 3 * HC, :].rearrange("p (w c) d -> p w c d", w=3)
        o_sb = extra[:, 2 + 3 * HC:2 + 4 * HC, :]

        w1_sb = [sb(f"w1_sb{c}", [2, HC, I]) for c in range(2)]
        w2_sb = [sb(f"w2_sb{c}", [2, H]) for c in range(2)]
        w2r_sb = [sb(f"w2r_sb{c}", [2, 2, H]) for c in range(2)]
        idx_sb = [[sb(f"idx_sb{c}{i}", [2], U32) for i in range(2)] for c in range(2)]

        used = {0: 0, 1: 0}

        def room(which, n):
            space = (space_a, space_b)[which]
            start = used[which]
            used[which] = start + n
            assert used[which] <= NT * RA * E // 2
            return space[:, start:start + n]

        y_sb = [room(0, 4 * H).rearrange("p (i s d) -> p i s d", i=2, s=2) for _ in range(2)]
        xg = [[room(0, 2 * H).rearrange("p (s d) -> p s d", s=2) for _ in range(2)] for _ in range(2)]
        hid = [room(0, 3 * P) for _ in range(2)]
        th = [room(0, 3 * P) for _ in range(2)]
        xg_t = [room(0, HC * SLOTS).rearrange("p (c s) -> p c s", c=HC) for _ in range(2)]

        used[0] = 0
        yg = [room(0, 2 * K * H).rearrange("p (s k d) -> p s k d", s=2, k=K) for _ in range(2)]
        z_sb = room(0, 2 * H).rearrange("p (s d) -> p s d", s=2)
        z_t = room(0, HC * S).rearrange("p (c s) -> p c s", c=HC)
        g_t = room(0, HC * S).rearrange("p (c s) -> p c s", c=HC)
        vo = room(1, 2 * H).rearrange("p (s d) -> p s d", s=2)
        scores = room(1, 3 * P)
        probs = room(1, 3 * P)
        probs_t = room(1, 3 * P)
        ffn = room(1, 2 * H).rearrange("p (s d) -> p s d", s=2)
        ffn_th = room(1, 2 * H)
        att = room(1, 2 * H)
        gated = room(1, 2 * H)
        out_sb = [room(1, 2 * H) for _ in range(2)]
        row_max = sb("row_max", [2])
        row_bias = sb("row_bias", [2])
        row_sum = sb("row_sum", [2])
        row_inv = sb("row_inv", [2])
        yi_sb = [sb(f"yi_sb{i}", [2, 8], U32) for i in range(2)]
        wk_sb = sb("wk_sb", [2, 8])

        x_in = [sem(f"x_in{g}") for g in range(GROUPS)]
        qkv_in, o_in, gb_in, gate_in, up_in = sem("qkv_in"), sem("o_in"), sem("gb_in"), sem("gate_in"), sem("up_in")
        pool_const, dve_const = sem("pool_const"), sem("dve_const")
        const_ready = sem("const_ready")
        wqk_done, wqk_ready = sem("wqk_done"), sem("wqk_ready")
        ln_step, var_ready, rstd_step, rstd_ready = sem("ln_step"), sem("var_ready"), sem("rstd_step"), sem("rstd_ready")
        xn_ready, xn_stored = sem("xn_ready"), sem("xn_stored")
        xnt_done, xnt_ready = sem("xnt_done"), sem("xnt_ready")
        logits_done, logits_ready, top_ready = sem("logits_done"), sem("logits_ready"), sem("top_ready")
        route_step, chosen_ready, exp_ready = sem("route_step"), sem("chosen_ready"), sem("exp_ready")
        before_step, rank_done, count_done = sem("before_step"), sem("rank_done"), sem("count_done")
        count_read, most_ready, rank_step, rank_ready = sem("count_read"), sem("most_ready"), sem("rank_step"), sem("rank_ready")
        hot_b_ready, hot_b_scaled, hot_a_ready, hot_a_read = sem("hot_b_ready"), sem("hot_b_scaled"), sem("hot_a_ready"), sem("hot_a_read")
        own_step, spread_ready, spread_done, slots_ready = (sem(n) for n in ("own_step", "spread_ready", "spread_done", "slots_ready"))
        idx_ready, xg_in = [sems("idx_ready0"), sems("idx_ready1")], [sems("xg_in0"), sems("xg_in1")]
        xg_t_done, xg_t_ready = [sems("xg_t_done0"), sems("xg_t_done1")], sems("xg_t_ready")
        w1_in, w2_in, w2r_clear = sems("w1_in"), sems("w2_in"), sem("w2r_clear")
        up_done, th_ready, hid_ready, y_done, y_ready, y_stored = (sems(n) for n in ("up_done", "th_ready", "hid_ready", "y_done", "y_ready", "y_stored"))
        fin_step, fin_done = sem("fin_step"), sem("fin_done")
        rounds_done, extra_idx_ready, extra_in, extra_step, extra_done = (
            sem(n) for n in ("rounds_done", "extra_idx_ready", "extra_in", "extra_step", "extra_done"))
        round_stored, extra_clear = sem("round_stored"), sem("extra_clear")
        gathers_begun, stores_begun, hot_a_begun = sem("gathers_begun"), sem("stores_begun"), sem("hot_a_begun")
        stats2_step, var2_ready, rstd2_step, shift2_ready = (sem(n) for n in ("stats2_step", "var2_ready", "rstd2_step", "shift2_ready"))
        yi_ready, yg_in, yg_late, combined = sems("yi_ready"), sems("yg_in"), sems("yg_late"), sems("combined")
        z_ready, zt_done, zt_ready = sem("z_ready"), sem("zt_done"), sem("zt_ready")
        gt_done, gt_ready, vo_done, vo_ready = sem("gt_done"), sem("gt_ready"), sem("vo_done"), sem("vo_ready")
        scores_done, scores_read, max_ready, bias_ready, probs_ready = (
            sem(n) for n in ("scores_done", "scores_read", "max_ready", "bias_ready", "probs_ready"))
        inv_ready, pt_done, pt_ready, pv_done, pv_read = sem("inv_ready"), sem("pt_done"), sem("pt_ready"), sem("pv_done"), sem("pv_read")
        gu_done, tg_ready, hg_step, hs_ready = sem("gu_done"), sem("tg_ready"), sem("hg_step"), sem("hs_ready")
        down_done, down_read, routed_step, ffn_th_ready = sem("down_done"), sem("down_read"), sem("routed_step"), sem("ffn_th_ready")
        final_step, out_ready, out_stored = sem("final_step"), sems("out_ready"), sems("out_stored")

        x_tiles = x.rearrange("(t p) d -> p t d", p=P)
        xn_tiles = xn_rows.rearrange("(t p) d -> p t d", p=P)
        out_tiles = out.rearrange("(t p) d -> p t d", p=P)

        block = ctx.enter_context(nc.Block())

        def fullest(eng):
            eng.wait_ge(most_ready, 1)
            return eng.value_load(most_int[0:1, 0:1], min_val=1, max_val=T)

        def rounds(eng, experts, again):
            if eng is nc.gpsimd:
                experts(0)
                n = fullest(eng)
            else:
                n = fullest(eng)
                experts(0)
            with eng.If(n > SLOTS):
                with eng.Fori(1, ROUNDS) as r:
                    with eng.If(n > r * SLOTS):
                        again(r)

        def repeat(eng, r, count, body):
            first = int(isinstance(r, int))
            if first:
                body(0)
            with eng.Fori(first, count) as j:
                body(j)

        def batches(body, eng):
            body(0, 0, 0)
            body(1, 1, 0)
            with eng.Fori(1, NB // 2 - 1) as j:
                body(2 * j, 0, j - 1)
                body(2 * j + 1, 1, j)
            body(NB - 2, 0, NB // 2 - 2)
            body(NB - 1, 1, NB // 2 - 1)

        def in_extra(b):
            return isinstance(b, int) and b in (0, NB - 1)

        @block.sync
        def _(sp):
            for g in range(GROUPS):
                sp.dma_start(x_all[:, g * GT:(g + 1) * GT, :], x_tiles[:, g * GT:(g + 1) * GT, :]).then_inc(x_in[g], 16)
            sp.dma_start(up_sb[:], shared_up_t).then_inc(up_in, 16)
            for m in range(SC):
                sp.dma_start(down_sb[0:SW[m], m, :], shared_down_t[m * P:m * P + SW[m], :]).then_inc(up_in, 16)
            def load_w1(p, c, np):
                for i in range(2):
                    sp.wait_ge(up_done[i], np)
                sp.dma_start(w1_sb[c][:], w1_t[bass.ds(2 * p, 2), :, :, :].rearrange("o p c i -> p o c i")).then_inc(w1_in[c], 16)

            def load_w2(p, c, np):
                for i in range(2):
                    sp.wait_ge(y_done[i], np)
                sp.dma_start(w2_sb[c][:], w2_main[bass.ds(2 * p, 2), :, :].rearrange("o p d -> p o d")).then_inc(w2_in[c], 16)
                rest = w2_rest[bass.ds(2 * p, 2), :, :].rearrange("o p d -> p o d")
                sp.dma_start(w2r_sb[c][0:IR, :, 0, :], rest).then_inc(w2_in[c], 16)
                sp.dma_start(w2r_sb[c][64:64 + IR, :, 1, :], rest).then_inc(w2_in[c], 16)

            def store_y(p, c, np):
                for i in range(2):
                    sp.wait_ge(y_ready[i], np)
                rows = y_rows[bass.ds(2 * p * SLOTS, 2 * SLOTS), :].rearrange("(o t p) d -> p o t d", o=2, p=P)
                sp.dma_start(rows, y_sb[c][:]).then_inc(y_stored[c], 16)

            def first_weights(r):
                sp.wait_ge(w2r_clear, 2)
                for c in range(2):
                    load_w1(c, c, r * (E // 2))
                    load_w2(c, c, r * (E // 2))

            def experts(r):
                n0 = r * (E // 2)
                with sp.Fori(0, E // 4 - 1) as j:
                    for c in range(2):
                        load_w1(2 * j + 2 + c, c, n0 + 2 * j + c + 1)
                        load_w2(2 * j + 2 + c, c, n0 + 2 * j + c + 1)
                        store_y(2 * j + c, c, n0 + 2 * j + c + 1)
                for c in range(2):
                    store_y(E // 2 - 2 + c, c, n0 + E // 2 - 1 + c)
                sp.wait_ge(xn_stored, 16 * GROUPS)
                for c in range(2):
                    sp.wait_ge(y_stored[c], 16 * (E // 4) * (r + 1))
                sp.sem_inc(round_stored, 1)

            def again(r):
                first_weights(r)
                sp.wait_ge(extra_done, NT * r)
                sp.sem_inc(stores_begun, 1)
                experts(r)

            for g in range(GROUPS):
                sp.wait_ge(xn_ready, g + 1)
                sp.dma_start(xn_tiles[:, g * GT:(g + 1) * GT, :], xn_all[:, g * GT:(g + 1) * GT, :]).then_inc(xn_stored, 16)
            first_weights(0)
            for i in range(2):
                sp.sem_inc(out_stored[i], 16)
            rounds(sp, experts, again)
            sp.sem_inc(rounds_done, 1)

            with sp.Fori(0, NB // 2) as j:
                for i in range(2):
                    sp.wait_ge(out_ready[i], j + 1)
                    sp.dma_start(out_tiles[:, bass.ds(2 * (2 * j + i), 2), :],
                                 out_sb[i].rearrange("p (s d) -> p s d", s=2)).then_inc(out_stored[i], 16)
            for i in range(2):
                sp.wait_ge(out_stored[i], 16 * (NB // 2 + 1))
            sp.wait_ge(xn_stored, 16 * GROUPS)

        @block.gpsimd
        def _(pool):
            pool.memset(ident[:], 0.0).then_inc(pool_const, 1)
            pool.memset(ones[:], 1.0).then_inc(pool_const, 1)
            pool.memset(before[:], 1.0).then_inc(pool_const, 1)
            pool.memset(causal[:], 0.0).then_inc(pool_const, 1)
            pool.memset(minus_half[:], -0.5).then_inc(pool_const, 1)
            pool.memset(chosen_before[:, 0, :], 0.0).then_inc(pool_const, 1)
            pool.wait_ge(pool_const, 6)
            pool.affine_select(out=ident[:], in_=ident[:], compare_op=ALU.not_equal, fill=1.0, base=0,
                               pattern=[[-1, P]], channel_multiplier=1).then_inc(const_ready, 1)
            pool.affine_select(out=before[:], in_=before[:], compare_op=ALU.is_gt, fill=0.0, base=0,
                               pattern=[[1, P]], channel_multiplier=-1).then_inc(const_ready, 1)
            for m in (0, 2):
                pool.affine_select(out=causal[:, m * P:(m + 1) * P], in_=causal[:, m * P:(m + 1) * P],
                                   compare_op=ALU.is_ge, fill=-1.0e30, base=0,
                                   pattern=[[-1, P]], channel_multiplier=1).then_inc(const_ready, 1)

            pool.iota(int_a[:, 0:P], [[RA, RA], [0, EG]], base=-BIG, channel_multiplier=0).then_inc(const_ready, 1)
            pool.iota(rank_int[:, 0:P], [[1, RA], [0, EG]], base=0, channel_multiplier=0).then_inc(const_ready, 1)
            pool.iota(int_a[:, P:P + NT], [[P, NT]], base=0, channel_multiplier=1).then_inc(const_ready, 1)
            pool.iota(int_a[:, 2 * P:2 * P + ROUNDS], [[SLOTS, ROUNDS]], base=0, channel_multiplier=0).then_inc(const_ready, 1)
            pool.iota(int_a[:, 3 * P:3 * P + ROUNDS], [[1, ROUNDS]], base=-(BIG // SLOTS), channel_multiplier=0).then_inc(const_ready, 1)
            pool.iota(expert_row[:], [[SLOTS, E]], base=0, channel_multiplier=0).then_inc(const_ready, 1)

            def rstd_of(g):
                ts = slice(g * GT, (g + 1) * GT)
                pool.wait_ge(var_ready, g + 1)
                pool.tensor_scalar(var_eps[:, ts], mean_var[:, ts, 1], EPS, None, ALU.add).then_inc(rstd_step, 1)
                pool.tensor_scalar(minus_mean[:, ts], mean_var[:, ts, 0], -1.0, None, ALU.mult).then_inc(rstd_step, 1)
                pool.wait_ge(rstd_step, 3 * g + 2)
                pool.tensor_tensor(rstd[:, ts], var_eps[:, ts], minus_half[:, ts], ALU.pow).then_inc(rstd_step, 1)
                pool.wait_ge(rstd_step, 3 * g + 3)
                pool.tensor_tensor(shift[:, ts], minus_mean[:, ts], rstd[:, ts], ALU.mult).then_inc(rstd_ready, 1)

            def count_before(g):
                pool.wait_ge(chosen_ready, g + 1)
                for t in range(g * GT, (g + 1) * GT):
                    if t:
                        pool.wait_ge(before_step, t)
                    pool.tensor_tensor(chosen_before[:, t + 1, :], chosen_before[:, t, :], chosen[:, t, :],
                                       ALU.add).then_inc(before_step, 1)

            rstd_of(0)
            rstd_of(1)
            rstd_of(2)
            count_before(0)
            rstd_of(3)
            count_before(1)
            count_before(2)
            count_before(3)
            pool.wait_ge(wqk_done, 2)
            pool.memset(extra[:, 2:NT - 2, :], 0.0).then_inc(extra_clear, 1)

            def gather_x(e, c, i, n):
                pool.wait_ge(xg_in[c][i], 32 * n)
                pool.tensor_copy(idx_sb[c][i][:], slot_token[:, :, bass.ds(e, 1)].rearrange("p h o -> p (h o)")).then_inc(idx_ready[c][i], 1)
                pool.wait_ge(idx_ready[c][i], n + 1)
                pool.wait_ge(xg_t_done[c][i], n)
                pool.sem_inc(gathers_begun, 1)
                for h in range(2):
                    pool.indirect_dma_start(xg[c][i][:, h, :], None, xn_rows,
                                            bass.IndirectOffsetOnAxis(ap=idx_sb[c][i][:, h:h + 1], axis=0)).then_inc(xg_in[c][i], 16)

            def experts(r):
                pool.wait_ge(xn_stored, 16 * GROUPS)
                pool.wait_ge(slots_ready, r + 1)
                pool.sem_inc(gathers_begun, 1)

                def four(j):
                    for c in range(2):
                        for i in range(2):
                            gather_x(4 * j + 2 * c + i, c, i, r * (E // 4) + j)

                repeat(pool, r, E // 4, four)

            def gather_extra(r):
                with pool.Fori(0, NT) as t:
                    n = r * NT + t
                    pool.tensor_copy(yi_sb[0][:, 0:1, :], y_row[:, bass.ds(t, 1), :]).then_inc(extra_idx_ready, 1)
                    pool.wait_ge(extra_idx_ready, n + 1)
                    pool.wait_ge(round_stored, r + 1)
                    pool.sem_inc(gathers_begun, 1)
                    for k in range(K):
                        pool.indirect_dma_start(yg[0][:, 0, k, :], None, y_rows,
                                                bass.IndirectOffsetOnAxis(ap=yi_sb[0][:, 0, k:k + 1], axis=0)).then_inc(extra_in, 16)
                    pool.wait_ge(extra_done, n + 1)

            def again(r):
                gather_extra(r - 1)
                experts(r)

            rounds(pool, experts, again)

            pool.wait_ge(var2_ready, 1)
            pool.tensor_scalar(var_eps[:], mean_var2[:, :, 1], EPS, None, ALU.add).then_inc(rstd2_step, 1)
            pool.tensor_scalar(minus_mean[:], mean_var2[:, :, 0], -1.0, None, ALU.mult).then_inc(rstd2_step, 1)
            pool.wait_ge(rstd2_step, 2)
            pool.tensor_tensor(rstd2[:], var_eps[:], minus_half[:], ALU.pow).then_inc(rstd2_step, 1)
            pool.wait_ge(rstd2_step, 3)
            pool.tensor_tensor(shift2[:], minus_mean[:], rstd2[:], ALU.mult).then_inc(shift2_ready, 1)
            pool.wait_ge(fin_done, 1)
            pool.wait_ge(rounds_done, 1)

            def two_batches(j):
                for i in range(2):
                    pool.wait_ge(yg_in[i], (2 * K - LATE) * 16 * j)
                    pool.wait_ge(yg_late[i], LATE * 16 * j)
                    pool.tensor_copy(yi_sb[i][:], y_row[:, bass.ds(2 * (2 * j + i), 2), :]).then_inc(yi_ready[i], 1)
                    pool.wait_ge(yi_ready[i], j + 1)
                    if not (isinstance(j, int) and j == 0):
                        pool.wait_ge(routed_step, 2 * K * (2 * j + i - 2) + 2 * K - LATE + 1)
                    pool.sem_inc(gathers_begun, 1)
                    for q in range(2 * K):
                        if q == 2 * K - LATE:
                            pool.wait_ge(combined[i], j)
                            pool.sem_inc(gathers_begun, 1)
                        k, s = q // 2, q % 2
                        pool.indirect_dma_start(yg[i][:, s, k, :], None, y_rows,
                                                bass.IndirectOffsetOnAxis(ap=yi_sb[i][:, s, k:k + 1], axis=0)
                                                ).then_inc(yg_in[i] if q < 2 * K - LATE else yg_late[i], 16)

            repeat(pool, 0, NB // 2, two_batches)

        def exps(act, g):
            act.wait_ge(top_ready, g + 1)
            for t in range(g * GT, (g + 1) * GT):
                ins = act.activation(exp_all[:, t, :], logits[:, t, 0:E], ACT.Exp, bias=neg_max[:, t:t + 1])
            ins.then_inc(exp_ready, 1)

        @block.scalar
        def _(act):
            act.dma_start(gate_sb[:], gate_t).then_inc(gate_in, 16)
            act.dma_start(qkv_sb, qkv_t).then_inc(qkv_in, 16)
            act.dma_start(o_sb, o_proj.rearrange("(c p) n -> p c n", p=P)).then_inc(o_in, 16)
            act.dma_start(gb[:], gamma_beta).then_inc(gb_in, 16)

            def gate_tanh(v, c, m, src):
                q = SC * v + m
                act.wait_ge(gu_done, q + 1)
                if not isinstance(q, int) or q >= 2:
                    act.wait_ge(hs_ready, q - 1)
                act.activation(tg[c][0:SW[m], :], src[0:SW[m], 0:S], ACT.Tanh, scale=0.5).then_inc(tg_ready, 1)

            def scale_b(t, n):
                act.wait_ge(hot_b_ready, n + 1)
                act.activation(hot_b[:, bass.ds(t, 1), :, :, :].rearrange("p o g b e -> p (o g b e)"),
                               hot_b[:, bass.ds(t, 1), :, :, :].rearrange("p o g b e -> p (o g b e)"), ACT.Copy,
                               scale=token_no[:, bass.ds(t, 1)]).then_inc(hot_b_scaled, 1)

            def normalise(g):
                act.wait_ge(rstd_ready, g + 1)
                for t in range(g * GT, (g + 1) * GT):
                    ins = act.activation(xn_all[:, t, :], x_all[:, t, :], ACT.Identity, bias=shift[:, t:t + 1], scale=rstd[:, t:t + 1])
                ins.then_inc(xn_ready, 1)

            normalise(0)
            for g in range(GROUPS):
                for u in range(2):
                    act.wait_ge(xnt_done, 2 * g + u + 1)
                    t = g * GT + 2 * u
                    act.copy(xn_t[:, :, t * P:(t + 2) * P], bank[u][:].rearrange("p (c s) -> p c s", c=HC)).then_inc(xnt_ready, 1)
                if g < GROUPS - 1:
                    normalise(g + 1)
                if g:
                    exps(act, g - 1)
                if g == 2:
                    for w, dst in enumerate((wqk, wvo)):
                        act.wait_ge(wqk_done, w + 1)
                        act.copy(dst[:].rearrange("p c n -> p (c n)"), bank[6 + w][:]).then_inc(wqk_ready, 1)
            for t in range(NT):
                scale_b(t, t)
                if t in (7, 11, 13):
                    m = (7, 11, 13).index(t)
                    gate_tanh(0, m % 2, m, bank[m % 2])
            exps(act, GROUPS - 1)
            act.wait_ge(down_done, 1)
            act.activation(extra[:, 0:2, :].rearrange("p s d -> p (s d)"), bank[1][:], ACT.Copy, scale=0.5).then_inc(down_read, 1)
            for m in range(SC):
                gate_tanh(1, (SC + m) % 2, m, bank[7 - m % 2])

            def expert(c, i, n, m):
                act.wait_ge(xg_t_done[c][i], m + 1)
                act.wait_ge(up_done[i], n)
                act.copy(xg_t[i][:].rearrange("p c s -> p (c s)"), bank[i][:]).then_inc(xg_t_ready[i], 1)
                act.wait_ge(up_done[i], n + 1)
                act.wait_ge(hid_ready[i], n)
                act.activation(th[i][:], bank[2 + i][:, 0:3 * P], ACT.Tanh, scale=0.5).then_inc(th_ready[i], 1)

            def experts(r):
                def four(j):
                    for c in range(2):
                        for i in range(2):
                            expert(c, i, r * (E // 2) + 2 * j + c, r * (E // 4) + j)

                repeat(act, r, E // 4, four)

            def again(r):
                with act.Fori(0, NT) as t:
                    scale_b(t, NT * r + t)
                experts(r)

            rounds(act, experts, again)

            def z_of(b):
                act.wait_ge(zt_done, b)
                for s in range(2):
                    t = 2 * b + s
                    ins = act.activation(z_sb[:, s, :], xn_all[:, bass.ds(t, 1), :].rearrange("p o d -> p (o d)"),
                                         ACT.Identity, bias=shift2[:, bass.ds(t, 1)], scale=rstd2[:, bass.ds(t, 1)])
                ins.then_inc(z_ready, 1)

            def z_evac(b):
                act.wait_ge(zt_done, b + 1)
                act.wait_ge(scores_done, b)
                for c in range(HC):
                    ins = act.activation(z_t[:, c, :], bank[3][:, c * S:(c + 1) * S], ACT.Identity,
                                         bias=gb[:, 1, c:c + 1], scale=gb[:, 0, c:c + 1])
                ins.then_inc(zt_ready, 1)

            def g_evac(b):
                act.wait_ge(gt_done, b + 1)
                act.copy(g_t.rearrange("p c s -> p (c s)"), bank[1][:]).then_inc(gt_ready, 1)

            def vo_evac(b):
                act.wait_ge(vo_done, b + 1)
                act.wait_ge(pv_done, b)
                act.copy(vo.rearrange("p s d -> p (s d)"), bank[2][:]).then_inc(vo_ready, 1)

            def ffn_tanh(b, i, n):
                act.wait_ge(combined[i], n + 1)
                act.activation(ffn_th, ffn.rearrange("p s d -> p (s d)"), ACT.Tanh, scale=0.5).then_inc(ffn_th_ready, 1)

            def batch(b, i, n):
                first, last = (isinstance(b, int) and b == v for v in (0, NB - 1))
                act.wait_ge(bias_ready, b + 1)
                act.wait_ge(pt_done, b)
                act.wait_ge(inv_ready, b)
                act.activation(probs[:, 0:P], scores[:, 0:P], ACT.Exp, bias=row_bias[:, 0:1], scale=SCALE,
                               accum_out=row_sum[:, 0:1])
                act.activation(probs[:, P:3 * P], scores[:, P:3 * P], ACT.Exp, bias=row_bias[:, 1:2], scale=SCALE,
                               accum_out=row_sum[:, 1:2]).then_inc(probs_ready, 1)
                shared = not in_extra(b)
                for m in range(SC):
                    c = (SC * (1 - i) + m) % 2
                    if m == SC - 1 and not last:
                        z_evac(b + 1)
                    if shared:
                        gate_tanh(b + 1, c, m, bank[4 + c])
                act.wait_ge(pt_done, b + 1)
                act.copy(probs_t, bank[0][:, 0:3 * P]).then_inc(pt_ready, 1)
                if not (isinstance(b, int) and b >= NB - 2):
                    z_of(b + 2)
                if not last:
                    g_evac(b + 1)
                if not first:
                    ffn_tanh(b - 1, 1 - i, n)
                if not last:
                    vo_evac(b + 1)

            act.wait_ge(gb_in, 16)
            act.wait_ge(shift2_ready, 1)
            z_of(0)
            z_evac(0)
            z_of(1)
            g_evac(0)
            vo_evac(0)
            batches(batch, act)
            ffn_tanh(NB - 1, 1, NB // 2 - 1)

        @block.vector
        def _(dve):
            dve.memset(logits[:, :, E:E + 2], PAD).then_inc(dve_const, 1)
            dve.memset(taken[:, :, K:8], PAD).then_inc(dve_const, 1)
            for i in range(2):
                dve.memset(w2r_sb[i][:], 0.0).then_inc(w2r_clear, 1)
                dve.memset(bank[2 + i][:], 0.0).then_inc(dve_const, 1)
            N_CONST = 4
            ln = [0]

            def statistics(g):
                dve.wait_ge(x_in[g], 16)
                for i in range(GT):
                    ins = dve.bn_stats(stats[:, i, :], x_all[:, g * GT + i, :])
                ins.then_inc(ln_step, 1)
                ln[0] += 1
                dve.wait_ge(ln_step, ln[0])
                for i in range(GT):
                    ins = dve.bn_aggr(mean_var[:, g * GT + i, :], stats[:, i, :])
                ins.then_inc(var_ready, 1)
                dve.wait_ge(var_ready, g + 1)

            def by_group(ranks, t):
                return (ranks[:, bass.ds(t, 1), :].rearrange("p o (g e) -> p (o g) e", e=EG).unsqueeze(2)
                        .broadcast_to([P, E // EG, RA, EG]))

            def shared_hidden(v, c, m, src):
                q, w = SC * v + m, SW[m]
                dve.wait_ge(tg_ready, q + 1)
                if not isinstance(q, int) or q >= 2:
                    dve.wait_ge(hs_ready, q - 1)
                dve.scalar_tensor_tensor(out=hg[c][0:w, :], in0=tg[c][0:w, :], scalar=1.0, in1=src[0:w, 0:S],
                                         op0=ALU.add, op1=ALU.mult).then_inc(hg_step, 1)
                dve.wait_ge(hg_step, q + 1)
                dve.wait_ge(down_done, v)
                dve.tensor_tensor(hs[0:w, m, :], hg[c][0:w, :], src[0:w, S:2 * S], ALU.mult).then_inc(hs_ready, 1)

            rs = [0]

            def step(ins):
                rs[0] += 1
                ins.then_inc(route_step, 1)
                dve.wait_ge(route_step, rs[0])

            def route(g):
                ts = slice(g * GT, (g + 1) * GT)
                dve.wait_ge(logits_done, g + 1)
                dve.tensor_copy(logits[:, ts, 0:E], bank[2 + g % 2][:, 0:GT * E].rearrange("p (t e) -> p t e", e=E)).then_inc(logits_ready, 1)
                dve.wait_ge(logits_ready, g + 1)
                for t in range(g * GT, (g + 1) * GT):
                    ins = dve.max(top8[:, t, :], logits[:, t, 0:E])
                step(ins)
                dve.tensor_scalar(neg_max[:, ts], top8[:, ts, 0], -1.0, None, ALU.mult).then_inc(top_ready, 1)
                step(dve.tensor_copy(taken[:, ts, 0:K], top8[:, ts, 0:K]))
                for i in range(GT):
                    ins = dve.match_replace(left[:, i, :], taken[:, g * GT + i, :], logits[:, g * GT + i, :], GONE)
                step(ins)
                dve.tensor_tensor(chosen[:, ts, :], left[:, :, 0:E], logits[:, ts, 0:E], ALU.not_equal).then_inc(chosen_ready, 1)

            def rank(g):
                ts = slice(g * GT * E, (g + 1) * GT * E)
                flat = lambda a: a[:, g * GT:(g + 1) * GT, :].rearrange("p t e -> p (t e)")
                count = bank[4 + g // 2][:, (g % 2) * GT * E:(g % 2 + 1) * GT * E]
                dve.wait_ge(rank_done, g + 1)
                dve.scalar_tensor_tensor(out=rank_int[:, ts], in0=flat(chosen), scalar=-float(BIG), in1=count,
                                         op0=ALU.mult, op1=ALU.add).then_inc(rank_step, 1)
                dve.wait_ge(rank_step, 3 * g + 1)
                dve.tensor_scalar(int_a[:, ts], rank_int[:, ts], RA - 1, None, ALU.bitwise_and).then_inc(rank_step, 1)
                dve.wait_ge(rank_step, 3 * g + 2)
                dve.tensor_copy(flat(rank_b), int_a[:, ts])
                dve.tensor_tensor(flat(rank_a), rank_int[:, ts], int_a[:, ts], ALU.subtract).then_inc(rank_step, 1)

            def one_hot(t, ranks_a):
                dve.tensor_tensor(hot_b[:, bass.ds(t, 1), :, :, :].rearrange("p o g b e -> p (o g) b e"), by_group(rank_b, t),
                                  iota_b[:].unsqueeze(1).broadcast_to([P, E // EG, RA, EG]), ALU.is_equal).then_inc(hot_b_ready, 1)
                dve.tensor_tensor(hot_a[:, bass.ds(t, 1), :, :, :].rearrange("p o g a e -> p (o g) a e"), by_group(ranks_a, t),
                                  iota_a[:].unsqueeze(1).broadcast_to([P, E // EG, RA, EG]), ALU.is_equal).then_inc(hot_a_ready, 1)

            def one_hots(g):
                dve.wait_ge(rank_step, 3 * g + 3)
                for t in range(g * GT, (g + 1) * GT):
                    one_hot(t, rank_a)

            dve.wait_ge(dve_const, N_CONST)
            statistics(0)
            dve.wait_ge(const_ready, 10)
            dve.tensor_copy(iota_a[:].rearrange("p a e -> p (a e)"), int_a[:, 0:P]).then_inc(dve_const, 1)
            dve.tensor_copy(iota_b[:].rearrange("p a e -> p (a e)"), rank_int[:, 0:P]).then_inc(dve_const, 1)
            dve.tensor_copy(token_no[:], int_a[:, P:P + NT]).then_inc(dve_const, 1)
            dve.tensor_copy(round_a[:], int_a[:, 2 * P:2 * P + ROUNDS]).then_inc(dve_const, 1)
            dve.tensor_copy(round_q[:], int_a[:, 3 * P:3 * P + ROUNDS]).then_inc(dve_const, 1)
            dve.tensor_reduce(same_expert[:], ident[:].rearrange("p (a e) -> p e a", a=RA), AX_X, ALU.add).then_inc(dve_const, 1)
            dve.tensor_reduce(partition_a[:], ident[:].rearrange("p (a e) -> p a e", a=RA), AX_X, ALU.add).then_inc(dve_const, 1)
            statistics(1)
            dve.wait_ge(dve_const, N_CONST + 7)
            dve.tensor_copy(partition_e[:], same_expert[:]).then_inc(dve_const, 1)
            dve.tensor_copy(select_a[:], partition_a[:].unsqueeze(2).broadcast_to([P, RA, RA])).then_inc(dve_const, 1)
            statistics(2)
            route(0)
            statistics(3)
            dve.wait_ge(dve_const, N_CONST + 9)
            rank(0)
            route(1)
            one_hots(0)
            rank(1)
            route(2)
            one_hots(1)
            rank(2)
            route(3)
            shared_hidden(0, 0, 0, bank[0])
            one_hots(2)
            rank(3)
            shared_hidden(0, 1, 1, bank[1])
            one_hots(3)
            shared_hidden(0, 0, 2, bank[0])

            def hidden(i, n):
                dve.wait_ge(th_ready[i], n + 1)
                dve.wait_ge(y_done[i], n)
                dve.scalar_tensor_tensor(out=hid[i][:], in0=th[i][:], scalar=1.0, in1=bank[2 + i][:, 0:3 * P],
                                         op0=ALU.add, op1=ALU.mult).then_inc(hid_ready[i], 1)

            def y_evac(c, i, n, m):
                dve.wait_ge(y_done[i], n + 1)
                dve.wait_ge(y_stored[c], 16 * m)
                dve.tensor_copy(y_sb[c][:, i, :, :].rearrange("p s d -> p (s d)"), bank[4 + i][:]).then_inc(y_ready[i], 1)

            def finish(r, t, part):
                n = 6 * (NT * r + t)
                row = lambda a: a[:, bass.ds(t, 1), :].rearrange("p o e -> p (o e)")
                ranks = rank_int[:, bass.ds(t * E, E)]
                if part == 0:
                    dve.wait_ge(exp_ready, GROUPS)
                    dve.wait_ge(fin_step, n)
                    dve.scalar_tensor_tensor(out=f_w[:], in0=row(exp_all), scalar=1.0, in1=row(chosen),
                                             op0=ALU.mult, op1=ALU.mult, accum_out=f_sum[:])
                    dve.tensor_scalar(f_slot[:], ranks, SLOTS - 1, None, ALU.bitwise_and)
                    dve.tensor_scalar(f_q[:], ranks, SLOTS.bit_length() - 1, None, ALU.arith_shift_right).then_inc(fin_step, 1)
                    dve.wait_ge(fin_step, n + 1)
                    dve.reciprocal(f_inv[:], f_sum[:])
                    dve.scalar_tensor_tensor(out=f_k1[:], in0=row(chosen), scalar=ABOVE, in1=f_slot[:],
                                             op0=ALU.mult, op1=ALU.subtract).then_inc(fin_step, 1)
                    dve.wait_ge(fin_step, n + 2)
                    dve.tensor_tensor(f_key[:], f_k1[:], expert_row[:], ALU.subtract).then_inc(fin_step, 1)
                    return
                dve.wait_ge(fin_step, n + 3)
                dve.scalar_tensor_tensor(out=f_round_w[:], in0=f_q[:], scalar=round_q[:, bass.ds(r, 1)], in1=f_w[:],
                                         op0=ALU.is_equal, op1=ALU.mult)
                dve.max(f_top[:], f_key[:]).then_inc(fin_step, 1)
                dve.wait_ge(fin_step, n + 4)
                dve.tensor_scalar(row(y_row), f_top[:], -1.0, ABOVE, ALU.mult, ALU.add)
                for k in range(K):
                    ins = dve.scalar_tensor_tensor(out=f_hit[:, k, :], in0=f_key[:], scalar=f_top[:, k:k + 1], in1=f_round_w[:],
                                                   op0=ALU.is_equal, op1=ALU.mult, accum_out=f_wk[:, k:k + 1])
                ins.then_inc(fin_step, 1)
                dve.wait_ge(fin_step, n + 5)
                dve.tensor_scalar(row(weight)[:, 0:K], f_wk[:, 0:K], f_inv[:, 0:1], 0.5, ALU.mult, ALU.mult).then_inc(fin_step, 1)

            def place_slots(r):
                n = 4 * r
                for h in range(2):
                    dve.wait_ge(hot_a_read, 2 * r + h + 1)
                    dve.tensor_tensor(own[:, h * 512:(h + 1) * 512].rearrange("p (g e) -> p g e", e=EG),
                                      bank[6 + h][:].rearrange("p (g e) -> p g e", e=EG),
                                      same_expert[:].unsqueeze(1).broadcast_to([P, 64, EG]), ALU.mult).then_inc(own_step, 1)
                dve.wait_ge(own_step, n + 2)
                with nc.allow_low_precision(reason="one number below 2048 among zeros"):
                    dve.tensor_reduce(lists[:], own[:].rearrange("p (g e) -> p g e", e=EG), AX_X, ALU.add).then_inc(own_step, 1)
                dve.wait_ge(own_step, n + 3)
                dve.tensor_tensor(spread, lists[:].rearrange("p (g b) -> p g b", g=E // EG).unsqueeze(2).broadcast_to([P, E // EG, RA, RA]),
                                  select_a[:].unsqueeze(1).broadcast_to([P, E // EG, RA, RA]), ALU.mult).then_inc(spread_ready, 1)
                dve.wait_ge(spread_done, r + 1)
                dve.tensor_copy(slot_token[:], bank[6][:, 0:2 * E].rearrange("p (h e) -> p h e", h=2)).then_inc(slots_ready, 1)

            def experts(r):
                n0, m0 = r * (E // 2), r * (E // 4)
                hidden(0, n0)
                if isinstance(r, int):
                    dve.wait_ge(down_done, 2)
                    dve.tensor_scalar(extra[:, NT - 2:NT, :].rearrange("p s d -> p (s d)"), bank[6][:], 0.5, None, ALU.mult).then_inc(down_read, 1)

                def four(t):
                    for u in range(2):
                        if u:
                            finish(r, t, 0)
                        hidden(1, n0 + 2 * t + u)
                        y_evac(u, 0, n0 + 2 * t + u, m0 + t)
                        if not (isinstance(t, int) and t == NT - 1 and u == 1):
                            hidden(0, n0 + 2 * t + u + 1)
                        y_evac(u, 1, n0 + 2 * t + u, m0 + t)
                    finish(r, t, 1)

                def statistics2(t):
                    for u in range(2):
                        ins = dve.bn_stats(stats2[:, bass.ds(2 * t + u, 1), :].rearrange("p o d -> p (o d)"),
                                           xn_all[:, bass.ds(2 * t + u, 1), :].rearrange("p o d -> p (o d)"))
                    ins.then_inc(stats2_step, 1)

                if isinstance(r, int):
                    def four_and_statistics(t):
                        four(t)
                        statistics2(t)

                    repeat(dve, r, NT // 2, four_and_statistics)
                    dve.wait_ge(stats2_step, NT // 2)
                    for t in range(NT):
                        ins = dve.bn_aggr(mean_var2[:, t, :], stats2[:, t, :])
                    ins.then_inc(var2_ready, 1)
                    with dve.Fori(NT // 2, NT - 1) as t:
                        four(t)
                else:
                    with dve.Fori(0, NT - 1) as t:
                        four(t)
                four(NT - 1)

            def add_extra(r):
                dve.wait_ge(down_read, 2)
                dve.sem_inc(hot_a_begun, 1)
                with dve.Fori(0, NT) as t:
                    total = extra[:, bass.ds(t, 1), :].rearrange("p o d -> p (o d)")
                    n = r * NT + t
                    dve.wait_ge(extra_in, K * 16 * (n + 1))
                    dve.tensor_copy(wk_sb[:, 0:1, 0:K], weight[:, bass.ds(t, 1), 0:K]).then_inc(extra_step, 1)
                    for k in range(K):
                        dve.wait_ge(extra_step, K * n + k + 1)
                        dve.scalar_tensor_tensor(out=total, in0=yg[0][:, 0, k, :], scalar=wk_sb[:, 0, k:k + 1], in1=total,
                                                 op0=ALU.mult, op1=ALU.add).then_inc(extra_step if k < K - 1 else extra_done, 1)
                    dve.wait_ge(extra_done, n + 1)

            def again(r):
                add_extra(r - 1)
                dve.tensor_scalar(round_rank_a[:].rearrange("p t e -> p (t e)"), rank_a[:].rearrange("p t e -> p (t e)"),
                                  round_a[:, bass.ds(r, 1)], None, ALU.subtract).then_inc(own_step, 1)
                dve.wait_ge(own_step, 4 * r)
                dve.sem_inc(hot_a_begun, 1)
                with dve.Fori(0, NT) as t:
                    one_hot(t, round_rank_a)
                place_slots(r)
                experts(r)

            place_slots(0)
            dve.wait_ge(extra_clear, 1)
            dve.wait_ge(count_done, 1)
            dve.tensor_reduce(most[:], bank[2][:, 0:E], AX_X, ALU.max).then_inc(count_read, 1)
            dve.wait_ge(count_read, 1)
            dve.tensor_copy(most_int[:], most[:]).then_inc(most_ready, 1)
            for m in range(SC):
                shared_hidden(1, (SC + m) % 2, m, bank[7 - m % 2])
            rounds(dve, experts, again)
            dve.memset(wk_sb[:], 0.0).then_inc(fin_done, 1)

            def softmax_head(b):
                dve.wait_ge(scores_done, b + 1)
                dve.wait_ge(probs_ready, b)
                dve.tensor_tensor(scores, bank[3][:, 0:3 * P], causal[:], ALU.add).then_inc(scores_read, 1)
                dve.wait_ge(scores_read, b + 1)
                dve.tensor_reduce(row_max[:, 0:1], scores[:, 0:P], AX_X, ALU.max)
                dve.tensor_reduce(row_max[:, 1:2], scores[:, P:3 * P], AX_X, ALU.max).then_inc(max_ready, 1)
                dve.wait_ge(max_ready, b + 1)
                dve.tensor_scalar(row_bias[:], row_max[:], -SCALE, None, ALU.mult).then_inc(bias_ready, 1)

            def add_shared(b):
                dve.wait_ge(ffn_th_ready, b)
                dve.wait_ge(final_step, 2 * b)
                if not in_extra(b):
                    dve.wait_ge(down_done, b + 2)
                    dve.scalar_tensor_tensor(out=ffn.rearrange("p s d -> p (s d)"), in0=bank[7][:], scalar=0.5,
                                             in1=extra[:, bass.ds(2 * b, 2), :].rearrange("p s d -> p (s d)"),
                                             op0=ALU.mult, op1=ALU.add).then_inc(down_read, 1)
                dve.tensor_copy(wk_sb[:, :, 0:K], weight[:, bass.ds(2 * b, 2), 0:K]).then_inc(routed_step, 1)

            def combine(b, i, n, rows):
                before = 2 * K * b
                for q in rows:
                    k, s = q // 2, q % 2
                    if q == 0:
                        dve.wait_ge(yg_in[i], (2 * K - LATE) * 16 * (n + 1))
                        if not in_extra(b):
                            dve.wait_ge(down_read, b + 2)
                    if q == 2 * K - LATE:
                        dve.wait_ge(yg_late[i], LATE * 16 * (n + 1))
                    dve.wait_ge(routed_step, before + max(q, 1))
                    dve.scalar_tensor_tensor(out=ffn[:, s, :], in0=yg[i][:, s, k, :], scalar=wk_sb[:, s, k:k + 1],
                                             in1=extra[:, 2 * b + s, :] if in_extra(b) and q < 2 else ffn[:, s, :],
                                             op0=ALU.mult, op1=ALU.add
                                             ).then_inc(combined[i] if q == 2 * K - 1 else routed_step, 1)

            def attended(b):
                dve.wait_ge(pv_done, b + 1)
                for s in range(2):
                    ins = dve.scalar_tensor_tensor(out=att[:, s * H:(s + 1) * H], in0=bank[6][:, s * H:(s + 1) * H],
                                                   scalar=row_inv[:, s:s + 1],
                                                   in1=xn_all[:, bass.ds(2 * b + s, 1), :].rearrange("p o d -> p (o d)"),
                                                   op0=ALU.mult, op1=ALU.add)
                ins.then_inc(pv_read, 1)

            def inverse(b):
                dve.wait_ge(probs_ready, b + 1)
                dve.wait_ge(pv_read, b)
                dve.reciprocal(row_inv[:], row_sum[:]).then_inc(inv_ready, 1)

            def final(b, i, n):
                dve.wait_ge(combined[i], n + 1)
                dve.wait_ge(pv_read, b + 1)
                dve.tensor_tensor(gated, ffn.rearrange("p s d -> p (s d)"), att, ALU.mult).then_inc(final_step, 1)
                dve.wait_ge(ffn_th_ready, b + 1)
                dve.wait_ge(final_step, 2 * b + 1)
                dve.scalar_tensor_tensor(out=gated, in0=ffn_th, scalar=1.0, in1=gated, op0=ALU.add, op1=ALU.mult).then_inc(final_step, 1)
                dve.wait_ge(final_step, 2 * b + 2)
                dve.wait_ge(out_stored[i], 16 * (n + 1))
                dve.scalar_tensor_tensor(out=out_sb[i], in0=gated, scalar=0.5,
                                         in1=x_all[:, bass.ds(2 * b, 2), :].rearrange("p s d -> p (s d)"),
                                         op0=ALU.mult, op1=ALU.add).then_inc(out_ready[i], 1)

            def batch(b, i, n):
                first = isinstance(b, int) and b == 0
                pb, pi = b - 1, 1 - i

                def hidden_here(m):
                    if not in_extra(b):
                        c = (SC * (1 - i) + m) % 2
                        shared_hidden(b + 1, c, m, bank[4 + c])

                last = isinstance(b, int) and b == NB - 1
                if last:
                    add_shared(pb)
                    combine(pb, pi, n, range(0, AHEAD))
                softmax_head(b)
                if last:
                    attended(pb)
                    combine(pb, pi, n, range(AHEAD, 2 * K))
                    inverse(b)
                    dve.wait_ge(inv_ready, b + 1)
                    final(pb, pi, n)
                    return
                if not first:
                    add_shared(pb)
                hidden_here(0)
                if not first:
                    attended(pb)
                    combine(pb, pi, n, range(0, 3))
                hidden_here(1)
                if not first:
                    combine(pb, pi, n, range(3, 6))
                hidden_here(2)
                if not first:
                    combine(pb, pi, n, range(6, 2 * K))
                inverse(b)
                dve.wait_ge(inv_ready, b + 1)
                if not first:
                    final(pb, pi, n)

            dve.wait_ge(down_read, 2)
            batches(batch, dve)
            add_shared(NB - 1)
            combine(NB - 1, 1, NB // 2 - 1, range(0, 2 * K - LATE))
            attended(NB - 1)
            combine(NB - 1, 1, NB // 2 - 1, range(2 * K - LATE, 2 * K))
            final(NB - 1, 1, NB // 2 - 1)

        @block.tensor
        def _(pe):
            def product(t, first=False, last=False):
                for g in range(E // EG):
                    ins = pe.matmul(bank[6 + g // 4][:, (g % 4) * P:(g % 4 + 1) * P],
                                    hot_a[:, bass.ds(t, 1), g, :, :].rearrange("p o a e -> p (o a e)"),
                                    hot_b[:, bass.ds(t, 1), g, :, :].rearrange("p o b e -> p (o b e)"),
                                    start=first and g % 4 == 0, stop=last, skip_group_check=True)
                    if last and g % 4 == 3:
                        ins.then_inc(hot_a_read, 1)

            def rank(g):
                dst = bank[4 + g // 2][:, (g % 2) * GT * E:(g % 2 + 1) * GT * E]
                pe.wait_ge(chosen_ready, g + 1)
                pe.matmul(dst, before[:], chosen[:, g * GT:(g + 1) * GT, :].rearrange("p t e -> p (t e)"), start=True, stop=False)
                pe.wait_ge(before_step, (g + 1) * GT - 1)
                pe.matmul(dst, ones[:], chosen_before[:, g * GT:(g + 1) * GT, :].rearrange("p t e -> p (t e)"),
                          start=False, stop=True).then_inc(rank_done, 1)

            def products(g):
                for t in range(g * GT, (g + 1) * GT):
                    pe.wait_ge(hot_b_scaled, t + 1)
                    pe.wait_ge(hot_a_ready, t + 1)
                    product(t, first=t == 0, last=t == NT - 1)

            pe.wait_ge(const_ready, 4)
            pe.wait_ge(gate_in, 16)
            def logits_of(g):
                pe.wait_ge(xn_ready, g + 1)
                for u in range(2):
                    if g:
                        pe.wait_ge(xnt_ready, 2 * (g - 1) + u + 1)
                    for v in range(2):
                        for c in range(HC):
                            ins = pe.transpose(bank[u][:, c * 2 * P + v * P:c * 2 * P + (v + 1) * P],
                                               xn_all[:, g * GT + 2 * u + v, c * P:(c + 1) * P], ident[:])
                    ins.then_inc(xnt_done, 1)
                if g >= 2:
                    pe.wait_ge(logits_ready, g - 1)
                for i in range(GT):
                    t = g * GT + i
                    pe.wait_ge(xnt_ready, 2 * g + i // 2 + 1)
                    for c in range(HC):
                        ins = pe.matmul(bank[2 + g % 2][:, i * E:(i + 1) * E], xn_t[:, c, t * P:(t + 1) * P],
                                        gate_sb[:, c, :], start=c == 0, stop=c == HC - 1)
                ins.then_inc(logits_done, 1)

            def weights_product(w):
                left_w = qkv_sb[:, (0, 2)[w], :, :]
                right_w = (qkv_sb[:, 1, :, :], o_sb)[w]
                for m in range(HC):
                    for k in range(HC):
                        ins = pe.matmul(bank[6 + w][:, m * H:(m + 1) * H], left_w[:, k, m * P:(m + 1) * P],
                                        right_w[:, k, :], start=k == 0, stop=k == HC - 1)
                ins.then_inc(wqk_done, 1)

            def gate_up(v, c, m, dst):
                q = SC * v + m
                b = (0, NB - 1)[v] if isinstance(v, int) and v < 2 else v - 1
                if not isinstance(q, int) or q >= 2:
                    pe.wait_ge(hs_ready, q - 1)
                for part in range(2):
                    for k in range(HC):
                        ins = pe.matmul(dst[0:SW[m], part * S:(part + 1) * S],
                                        up_sb[:, k, part * SI + m * P:part * SI + m * P + SW[m]],
                                        xn_t[:, k, bass.ds(b * S, S)], start=k == 0, stop=k == HC - 1)
                ins.then_inc(gu_done, 1)

            def shared_down(v, dst):
                pe.wait_ge(hs_ready, SC * (v + 1))
                pe.wait_ge(down_read, v)
                for s in range(2):
                    for m in range(SC):
                        ins = pe.matmul(dst[:, s * H:(s + 1) * H], hs[0:SW[m], m, s * P:(s + 1) * P],
                                        down_sb[0:SW[m], m, :], start=m == 0, stop=m == SC - 1)
                ins.then_inc(down_done, 1)

            logits_of(0)
            logits_of(1)
            rank(0)
            logits_of(2)
            pe.wait_ge(qkv_in, 16)
            pe.wait_ge(o_in, 16)
            weights_product(0)
            weights_product(1)
            rank(1)
            logits_of(3)
            rank(2)
            pe.wait_ge(wqk_ready, 2)
            products(0)
            pe.wait_ge(up_in, 16 * (1 + SC))
            pe.wait_ge(xnt_ready, 2 * GROUPS)
            gate_up(0, 0, 0, bank[0])
            products(1)
            rank(3)
            gate_up(0, 1, 1, bank[1])
            products(2)
            gate_up(0, 0, 2, bank[0])
            products(3)
            def place_slots(r):
                pe.wait_ge(spread_ready, r + 1)
                for h in range(2):
                    for g in range(E // EG):
                        ins = pe.matmul(bank[6][:, h * E + g * EG:h * E + (g + 1) * EG],
                                        spread[:, g, h * RA // 2:(h + 1) * RA // 2, :].rearrange("p a b -> p (a b)"),
                                        partition_e[:], start=True, stop=True)
                ins.then_inc(spread_done, 1)

            def transpose_x(c, i, n, m):
                pe.wait_ge(xg_in[c][i], 32 * (m + 1))
                pe.wait_ge(xg_t_ready[i], n)
                for h in range(2):
                    for k in range(HC):
                        ins = pe.transpose(bank[i][:, k * SLOTS + h * P:k * SLOTS + (h + 1) * P],
                                           xg[c][i][:, h, k * P:(k + 1) * P], ident[:])
                ins.then_inc(xg_t_done[c][i], 1)

            def up(c, i, n, m):
                pe.wait_ge(w1_in[c], 16 * (m + 1))
                pe.wait_ge(xg_t_ready[i], n + 1)
                pe.wait_ge(hid_ready[i], n)
                for k in range(HC):
                    pe.matmul(bank[2 + i][:, 0:SLOTS], w1_sb[c][:, i, k, 0:P], xg_t[i][:, k, :], start=k == 0, stop=k == HC - 1)
                for k in range(HC):
                    for h in range(2):
                        ins = pe.matmul(bank[2 + i][64 * h:64 * h + IR, SLOTS:SLOTS + P], w1_sb[c][:, i, k, P:I],
                                        xg_t[i][:, k, h * P:(h + 1) * P], start=k == 0, stop=k == HC - 1,
                                        skip_group_check=True)
                ins.then_inc(up_done[i], 1)

            def down(c, i, n, m):
                pe.wait_ge(w2_in[c], 48 * (m + 1))
                pe.wait_ge(hid_ready[i], n + 1)
                pe.wait_ge(y_ready[i], n)
                for h in range(2):
                    pe.matmul(bank[4 + i][:, h * H:(h + 1) * H], hid[i][:, h * P:(h + 1) * P], w2_sb[c][:, i, :], start=True, stop=False)
                    ins = pe.matmul(bank[4 + i][:, h * H:(h + 1) * H], hid[i][:, SLOTS:SLOTS + P], w2r_sb[c][:, i, h, :],
                                    start=False, stop=True)
                ins.then_inc(y_done[i], 1)

            def experts(r):
                n0, m0 = r * (E // 2), r * (E // 4)

                def steps(j, c, last=False):
                    n, m = n0 + 2 * j + c, m0 + j
                    d, m_next = 1 - c, m0 + j + c
                    up(c, 1, n, m)
                    if not last:
                        transpose_x(d, 0, n + 1, m_next)
                    down(c, 0, n, m)
                    if not last:
                        up(d, 0, n + 1, m_next)
                        transpose_x(d, 1, n + 1, m_next)
                    down(c, 1, n, m)

                transpose_x(0, 0, n0, m0)
                up(0, 0, n0, m0)
                transpose_x(0, 1, n0, m0)
                if isinstance(r, int):
                    shared_down(1, bank[6])
                def four(j):
                    steps(j, 0)
                    steps(j, 1)

                repeat(pe, r, E // 4 - 1, four)
                steps(E // 4 - 1, 0)
                steps(E // 4 - 1, 1, last=True)
                for i in range(2):
                    pe.wait_ge(xg_t_ready[i], n0 + E // 2)
                    pe.wait_ge(hid_ready[i], n0 + E // 2)

            def again(r):
                pe.wait_ge(hot_b_scaled, NT * r + 1)
                pe.wait_ge(hot_a_ready, NT * r + 1)
                product(0, first=True)
                with pe.Fori(1, NT - 1) as t:
                    pe.wait_ge(hot_b_scaled, NT * r + t + 1)
                    pe.wait_ge(hot_a_ready, NT * r + t + 1)
                    product(t)
                pe.wait_ge(hot_b_scaled, NT * (r + 1))
                pe.wait_ge(hot_a_ready, NT * (r + 1))
                product(NT - 1, last=True)
                place_slots(r)
                experts(r)

            pe.wait_ge(before_step, NT)
            pe.wait_ge(logits_ready, GROUPS)
            pe.matmul(bank[2][:, 0:E], ones[:], chosen_before[:, NT, :], start=True, stop=True).then_inc(count_done, 1)

            shared_down(0, bank[1])
            place_slots(0)
            gate_up(1, 1, 0, bank[7])
            pe.wait_ge(slots_ready, 1)
            gate_up(1, 0, 1, bank[6])
            gate_up(1, 1, 2, bank[7])
            pe.wait_ge(down_read, 1)
            pe.wait_ge(count_read, 1)
            rounds(pe, experts, again)

            def transpose_z(b):
                pe.wait_ge(z_ready, b + 1)
                pe.wait_ge(scores_read, b)
                for s in range(2):
                    for c in range(HC):
                        ins = pe.transpose(bank[3][:, c * S + s * P:c * S + (s + 1) * P], z_sb[:, s, c * P:(c + 1) * P], ident[:])
                ins.then_inc(zt_done, 1)

            def g_of(b):
                pe.wait_ge(zt_ready, b + 1)
                pe.wait_ge(gt_ready, b)
                for m in range(HC):
                    for k in range(HC):
                        ins = pe.matmul(bank[1][:, m * S:(m + 1) * S], wqk[:, k, m * P:(m + 1) * P], z_t[:, k, :],
                                        start=k == 0, stop=k == HC - 1)
                ins.then_inc(gt_done, 1)

            def vo_of(b):
                pe.wait_ge(vo_ready, b)
                for s in range(2):
                    for k in range(HC):
                        ins = pe.matmul(bank[2][:, s * H:(s + 1) * H], z_t[:, k, s * P:(s + 1) * P], wvo[:, k, :],
                                        start=k == 0, stop=k == HC - 1)
                ins.then_inc(vo_done, 1)

            def scores_of(b):
                pe.wait_ge(gt_ready, b + 1)
                for s in range(2):
                    cols = (slice(0, P), slice(P, 3 * P))[s]
                    for k in range(HC):
                        ins = pe.matmul(bank[3][:, cols], g_t[:, k, s * P:(s + 1) * P], z_t[:, k, 0:(s + 1) * P],
                                        start=k == 0, stop=k == HC - 1)
                ins.then_inc(scores_done, 1)

            def transpose_probs(b):
                pe.wait_ge(probs_ready, b + 1)
                pe.wait_ge(pt_ready, b)
                for m in range(3):
                    ins = pe.transpose(bank[0][:, m * P:(m + 1) * P], probs[:, m * P:(m + 1) * P], ident[:])
                ins.then_inc(pt_done, 1)

            def attend(b):
                pe.wait_ge(pt_ready, b + 1)
                pe.wait_ge(vo_ready, b + 1)
                pe.wait_ge(pv_read, b)
                pe.matmul(bank[6][:, 0:H], probs_t[:, 0:P], vo[:, 0, :], start=True, stop=True)
                pe.matmul(bank[6][:, H:2 * H], probs_t[:, P:2 * P], vo[:, 0, :], start=True, stop=False)
                pe.matmul(bank[6][:, H:2 * H], probs_t[:, 2 * P:3 * P], vo[:, 1, :], start=False, stop=True).then_inc(pv_done, 1)

            def batch(b, i, n):
                last = isinstance(b, int) and b == NB - 1
                shared = not in_extra(b)
                for m in range(SC):
                    c = (SC * (1 - i) + m) % 2
                    if m == SC - 1 and not last:
                        transpose_z(b + 1)
                    if shared:
                        gate_up(b + 1, c, m, bank[4 + c])
                if shared or last:
                    transpose_probs(b)
                if not last:
                    g_of(b + 1)
                if not (shared or last):
                    transpose_probs(b)
                    vo_of(b + 1)
                attend(b)
                if shared:
                    shared_down(b + 1, bank[7])
                    vo_of(b + 1)
                if not last:
                    scores_of(b + 1)

            transpose_z(0)
            g_of(0)
            vo_of(0)
            scores_of(0)
            batches(batch, pe)


def kernel(L0_attn_x, L0_attn_qkv, L0_attn_o_proj, L0_attn_gamma, L0_attn_beta, L0_ffn_gate_w,
           L0_ffn_experts_w1, L0_ffn_experts_w2, L0_ffn_shared_gate_up, L0_ffn_shared_down):
    import numpy as np
    import concourse.bacc as bacc
    from concourse.bass_utils import run_bass_kernel_spmd

    x = np.asarray(L0_attn_x)
    B, S, H = x.shape
    HC = H // P
    qkv = np.asarray(L0_attn_qkv)
    w1 = np.asarray(L0_ffn_experts_w1)
    w2 = np.asarray(L0_ffn_experts_w2)
    E, I, _ = w1.shape
    w2t = w2.transpose(0, 2, 1)
    up = np.asarray(L0_ffn_shared_gate_up)
    arrays = {
        "x_rows": x.reshape(B * S, H),
        "qkv_t": qkv.reshape(H, 3, HC, P).transpose(3, 1, 2, 0),
        "o_proj": np.asarray(L0_attn_o_proj),
        "gamma_beta": np.stack([np.asarray(L0_attn_gamma), np.asarray(L0_attn_beta)]).reshape(2, HC, P).transpose(2, 0, 1),
        "gate_t": np.asarray(L0_ffn_gate_w).reshape(E, HC, P).transpose(2, 1, 0),
        "w1_t": w1.reshape(E, I, HC, P).transpose(0, 3, 2, 1),
        "w2_main": w2t[:, 0:P, :],
        "w2_rest": w2t[:, P:I, :],
        "shared_up_t": up.reshape(-1, HC, P).transpose(2, 1, 0),
        "shared_down_t": np.asarray(L0_ffn_shared_down).T,
    }
    arrays = {f"in_{k}": np.ascontiguousarray(v) for k, v in arrays.items()}
    nc = bacc.Bacc("TRN2", target_bir_lowering=False, num_devices=1)
    args = [nc.dram_tensor(k, v.shape, mybir.dt.from_np(v.dtype), kind="ExternalInput").ap() for k, v in arrays.items()]
    out = nc.dram_tensor("out_rows", (B * S, H), F32, kind="ExternalOutput").ap()
    gated_moe_attention(nc, *args, out)
    r = run_bass_kernel_spmd(nc, [arrays], core_ids=[0])
    return r.results[0]["out_rows"].reshape(B, S, H)
```
